# Optimizing a Trainium2 kernel written in Bass

```python
import numpy as np
import jax
import jax.numpy as jnp

def _softmax(x, axis=-1):
    return jax.nn.softmax(x, axis=axis)

def _gelu(x):
    return jax.nn.gelu(x, approximate=True)

def _silu(x):
    return jax.nn.silu(x)

def _sigmoid(x):
    return jax.nn.sigmoid(x)

def _layernorm(x, axis=-1, eps=1e-05):
    m = jnp.mean(x, axis=axis, keepdims=True)
    v = jnp.var(x, axis=axis, keepdims=True)
    return (x - m) / jnp.sqrt(v + eps)

def _scatter_add(tgt, idx, src, axis=0):
    return tgt.at[idx].add(src)

def _segment_sum(src, seg, n):
    return jax.ops.segment_sum(src, seg, n)
kernel_name = 'mk_xattn_ffn_d1_seqx_r4_0c28ee'

def setup_inputs(seed: int=0):
    np.random.seed(seed)
    _w = jnp.asarray

    def _rec_inputs():
        import jax
        import jax.numpy as jnp
        _rk = jax.random.key(seed)
        x = -0.0002928 + 1 * jax.random.normal(jax.random.fold_in(_rk, 1), (8, 256, 256), jnp.float32)
        _lenS = 256 - jax.random.randint(jax.random.fold_in(_rk, 7), (8,), 0, max(1, 256 // 4) + 1, jnp.int32)
        _lenS2 = 256 - jax.random.randint(jax.random.fold_in(_rk, 8), (8,), 0, max(1, 256 // 4) + 1, jnp.int32)
        _ctx_1024P = jax.random.normal(jax.random.fold_in(_rk, 11), (8, 16, 256), jnp.float32)
        _ctx_1024c = jax.random.dirichlet(jax.random.fold_in(_rk, 511), 0.3 * jnp.ones((16,), jnp.float32), (8, 256))
        _ctx_1024t = jnp.einsum('bsk,bkd->bsd', _ctx_1024c, _ctx_1024P)
        _ctx_1024t = _ctx_1024t * jax.lax.rsqrt(jnp.mean(jnp.square(_ctx_1024t)) + 1e-12) * 0.953939
        ctx_1024 = -1.39393e-06 + 0.999914 * (_ctx_1024t + 0.3 * jax.random.normal(jax.random.fold_in(_rk, 611), (8, 256, 256), jnp.float32))
        return (x, ctx_1024)
    x, ctx_1024 = _rec_inputs()

    def _L0_xattn_setup():
        import jax, jax.numpy as jnp
        import numpy as np
        DIM = 256
        NUM_HEADS = 16
        HEAD_DIM = DIM // NUM_HEADS
        key = jax.random.key(seed)
        ks = jax.random.split(key, 11)
        B, N, C = (2, 512, DIM)
        s = 1.0 / np.sqrt(C)
        inp = {'q': jax.random.normal(ks[0], (B, N, C), jnp.float32), 'k': jax.random.normal(ks[1], (B, N, C), jnp.float32), 'v': jax.random.normal(ks[2], (B, N, C), jnp.float32), 'Wq': jax.random.normal(ks[3], (C, C), jnp.float32) * s, 'bq': jnp.zeros((C,), jnp.float32), 'Wk': jax.random.normal(ks[4], (C, C), jnp.float32) * s, 'bk': jnp.zeros((C,), jnp.float32), 'Wv': jax.random.normal(ks[5], (C, C), jnp.float32) * s, 'bv': jnp.zeros((C,), jnp.float32), 'Wo': jax.random.normal(ks[6], (C, C), jnp.float32) * s, 'bo': jnp.zeros((C,), jnp.float32)}
        return inp
    _L0_xattn_all = _L0_xattn_setup()
    _L0_xattn_in = {k: v for k, v in _L0_xattn_all.items() if k in ('Wq', 'bq', 'Wk', 'bk', 'Wv', 'bv', 'Wo', 'bo')}
    del _L0_xattn_all

    def _L0_ffn_setup():
        import jax, jax.numpy as jnp
        import numpy as np
        B, S, H, M, E, K = (4, 512, 256, 1024, 8, 2)
        key = jax.random.key(seed)
        ks = jax.random.split(key, 6)
        x = jax.random.normal(ks[0], (B, S, H), dtype=jnp.float32)
        Wr = jax.random.normal(ks[1], (E, H), dtype=jnp.float32) * (1.0 / np.sqrt(H))
        W1 = jax.random.normal(ks[2], (E, M, H), dtype=jnp.float32) * np.sqrt(2.0 / (H + M))
        b1 = jax.random.normal(ks[3], (E, M), dtype=jnp.float32) * 1e-06
        W2 = jax.random.normal(ks[4], (E, H, M), dtype=jnp.float32) * np.sqrt(2.0 / (H + M))
        b2 = jax.random.normal(ks[5], (E, H), dtype=jnp.float32) * 1e-06
        return {'x': x, 'Wr': Wr, 'W1': W1, 'b1': b1, 'W2': W2, 'b2': b2}
    _L0_ffn_all = _L0_ffn_setup()
    _L0_ffn_in = {k: v for k, v in _L0_ffn_all.items() if k in ('Wr', 'W1', 'b1', 'W2', 'b2')}
    del _L0_ffn_all
    return {'x': x, 'ctx_1024': ctx_1024, 'L0_xattn_Wq': _L0_xattn_in['Wq'], 'L0_xattn_bq': _L0_xattn_in['bq'], 'L0_xattn_Wk': _L0_xattn_in['Wk'], 'L0_xattn_bk': _L0_xattn_in['bk'], 'L0_xattn_Wv': _L0_xattn_in['Wv'], 'L0_xattn_bv': _L0_xattn_in['bv'], 'L0_xattn_Wo': _L0_xattn_in['Wo'], 'L0_xattn_bo': _L0_xattn_in['bo'], 'L0_ffn_Wr': _L0_ffn_in['Wr'], 'L0_ffn_W1': _L0_ffn_in['W1'], 'L0_ffn_b1': _L0_ffn_in['b1'], 'L0_ffn_W2': _L0_ffn_in['W2'], 'L0_ffn_b2': _L0_ffn_in['b2']}

def reference(x, ctx_1024, L0_xattn_Wq, L0_xattn_bq, L0_xattn_Wk, L0_xattn_bk, L0_xattn_Wv, L0_xattn_bv, L0_xattn_Wo, L0_xattn_bo, L0_ffn_Wr, L0_ffn_W1, L0_ffn_b1, L0_ffn_W2, L0_ffn_b2):
    import jax
    import jax.numpy as jnp

    def _L0_xattn_ref(q, k, v, Wq, bq, Wk, bk, Wv, bv, Wo, bo):
        import jax, jax.numpy as jnp
        import numpy as np
        DIM = 256
        NUM_HEADS = 16
        HEAD_DIM = DIM // NUM_HEADS
        B, Nq, C = q.shape
        Nkv = k.shape[1]
        H, D = (NUM_HEADS, HEAD_DIM)
        qh = (q @ Wq.T + bq).reshape(B, Nq, H, D).transpose(0, 2, 1, 3)
        kh = (k @ Wk.T + bk).reshape(B, Nkv, H, D).transpose(0, 2, 1, 3)
        vh = (v @ Wv.T + bv).reshape(B, Nkv, H, D).transpose(0, 2, 1, 3)
        scale = D ** (-0.5)
        attn = jax.nn.softmax(jnp.einsum('bhqd,bhkd->bhqk', qh, kh) * scale, axis=-1)
        out = jnp.einsum('bhqk,bhkd->bhqd', attn, vh)
        out = out.transpose(0, 2, 1, 3).reshape(B, Nq, C)
        return out @ Wo.T + bo

    def _L0_ffn_ref(x, Wr, W1, b1, W2, b2):
        import jax, jax.numpy as jnp
        import numpy as np
        B, S, H, M, E, K = (4, 512, 256, 1024, 8, 2)
        logits = jnp.einsum('bsh,eh->bse', x, Wr)
        probs = jax.nn.softmax(logits, axis=-1)
        top_v, top_i = jax.lax.top_k(probs, K)
        top_v = top_v / jnp.sum(top_v, axis=-1, keepdims=True)
        out = jnp.zeros_like(x)
        for e in range(E):
            w_e = jnp.sum(jnp.where(top_i == e, top_v, 0.0), axis=-1)
            h = jnp.einsum('bsh,mh->bsm', x, W1[e]) + b1[e]
            h = jax.nn.gelu(h, approximate=False)
            y = jnp.einsum('bsm,hm->bsh', h, W2[e]) + b2[e]
            out = out + y * w_e[..., None]
        return out
    x = x + _L0_xattn_ref(_layernorm(x, axis=-1), ctx_1024, ctx_1024, L0_xattn_Wq, L0_xattn_bq, L0_xattn_Wk, L0_xattn_bk, L0_xattn_Wv, L0_xattn_bv, L0_xattn_Wo, L0_xattn_bo)
    x = x + _L0_ffn_ref(_layernorm(x, axis=-1), L0_ffn_Wr, L0_ffn_W1, L0_ffn_b1, L0_ffn_W2, L0_ffn_b2)
    return x

_drawn_inputs = setup_inputs


def setup_inputs(seed=0):
    import zlib

    import numpy as np

    out = dict(_drawn_inputs(seed))
    spreads = {'L0_xattn_bq': (0.0, 0.1),
     'L0_xattn_bk': (0.0, 0.1),
     'L0_xattn_bv': (0.0, 0.1),
     'L0_xattn_bo': (0.0, 0.1)}
    factors = {}
    for name, (base, spread) in spreads.items():
        noise = np.random.default_rng([zlib.crc32(name.encode()), seed]).standard_normal(out[name].shape)
        drawn = base * np.exp(spread * noise) if base else spread * noise
        out[name] = jnp.asarray(drawn.astype(out[name].dtype))
    for name, factor in factors.items():
        out[name] = (out[name] * factor).astype(out[name].dtype)
    return out
```

```python
import concourse.bass as bass
from concourse import mybir
from contextlib import ExitStack

B, N, C = 8, 256, 256
H = 16
D = C // H
E, M = 8, 1024
P = 128
KC = C // P
JT = N // P
MC = M // P
TOK = B * N
PAIRS = TOK * 2
NT = PAIRS // P + E - 1
REG = TOK + P
HR = 64
R3 = 3 * D
VW = D + 2
OW = D + 1
ROW = 272
R_ID, R_W = C, C + 1
EPS = 1e-5
XS, WS, HS = 1024.0, 512.0, 8.0
EW = 2 * 2 * KC * M
EH = EW // 2
CH = 1024
NCH = EH // CH
PRE = 6

LAG_ST, LAG_PV = 2, 4
SLOTS = H + LAG_PV
LN2, ROUTE = 5, 11
STEPS = B + 3


def cross_attention_moe(nc, x, ctxT, wqT, wkT, wvT, woT, bqk, bv, bo, wrT, w12, b1, b2, out):
    fp32, fp16, bf16 = mybir.dt.float32, mybir.dt.float16, mybir.dt.bfloat16
    i32, u32 = mybir.dt.int32, mybir.dt.uint32
    ALU, ACT, X = mybir.AluOpType, mybir.ActivationFunctionType, mybir.AxisListType.X
    ds = bass.ds

    q_st = nc.dram_tensor("q_stacked", (B, H, HR, N), fp16, kind="Internal").ap()
    k_st = nc.dram_tensor("k_stacked", (B, H, HR, N), fp16, kind="Internal").ap()
    routed = nc.dram_tensor("routed_rows", (E * REG + P, ROW), fp32, kind="Internal").ap()
    acc = nc.dram_tensor("accumulated", (TOK + P, C), fp32, kind="Internal").ap()

    with ExitStack() as ctx:
        def sb(name, shape, dt=fp32):
            return ctx.enter_context(nc.sbuf_tensor(name, shape, dt))

        Wx = sb("expert_weights", [P, E, EW], fp16)
        spare = Wx[:, PRE:E, :].rearrange("p e w -> p (e w)")
        NQ = 3 * H * N
        NV = 3 * JT * H * VW
        Qs = spare[:, 0:NQ].rearrange("p (r h n) -> p r h n", r=3, h=H)
        Vh = spare[:, NQ:NQ + NV].rearrange("p (r j h d) -> p r j h d", r=3, j=JT, h=H)
        Vl = spare[:, NQ + NV:NQ + 2 * NV].rearrange("p (r j h d) -> p r j h d", r=3, j=JT, h=H)

        AREA = 10240
        area = sb("area", [P, AREA])

        class Carve:
            def __init__(self):
                self.at = 0

            def __call__(self, words):
                self.at += words
                assert self.at <= AREA
                return area[:, self.at - words:self.at]

        a = Carve()
        Ks = a(3 * (H // 2) * N // 2).bitcast(fp16).rearrange("p (r h n) -> p r h n", r=3, h=H // 2)
        Pe = a(4 * JT * N).rearrange("p (r j n) -> p r j n", r=4, j=JT)
        Pl = a(4 * JT * N // 2).bitcast(fp16).rearrange("p (r j n) -> p r j n", r=4, j=JT)
        ctx_T = a(KC * N).rearrange("p (k n) -> p k n", k=KC)
        xnT = a(KC * N).rearrange("p (k n) -> p k n", k=KC)
        qk32 = a(KC * N).rearrange("p (k n) -> p k n", k=KC)
        k16 = a(KC * N).bitcast(fp16).rearrange("p (s k n) -> p s k n", s=2, k=KC)
        q16 = a(KC * N).bitcast(fp16).rearrange("p (s k n) -> p s k n", s=2, k=KC)
        VAT = a.at
        v32 = a(JT * C).rearrange("p (j c) -> p j c", j=JT)
        o_n = a(JT * C).rearrange("p (j c) -> p j c", j=JT)
        oT = a(KC * N).rearrange("p (k n) -> p k n", k=KC)
        used = a.at
        f = Carve()
        b2_bc = f(E * C).rearrange("p (e c) -> p e c", e=E)
        xr = f(2 * C).rearrange("p (r c) -> p r c", r=2)
        meta = f(2 * 16).rearrange("p (r c) -> p r c", r=2)
        xT = f(2 * 2 * KC * P // 2).bitcast(fp16).rearrange("p (r s n) -> p r s n", r=2, s=2 * KC)
        h32 = f(2 * M).rearrange("p (r m n) -> p r m n", r=2, m=MC)
        hh = f(M).bitcast(fp16).rearrange("p (r m n) -> p r m n", r=2, m=MC)
        hl = f(M).bitcast(fp16).rearrange("p (r m n) -> p r m n", r=2, m=MC)
        y = f(3 * C).rearrange("p (r c) -> p r c", r=3)
        assert f.at <= VAT and used <= AREA

        x_in = sb("x_in", [P, JT, C])
        xn = sb("x_normed", [P, JT, C])
        x_res = sb("x_residual", [P, JT, C])
        x1 = sb("x_attended", [P, JT, C])
        xn2 = sb("x_attended_normed", [P, JT, C])
        rows = sb("rows", [P, JT, ROW])
        rows16 = rows[:, :, :].bitcast(fp16)
        pad = sb("pad_row", [P, ROW])
        xt2 = sb("x_attended_T", [P, JT, 2 * KC, P], fp16)
        wq, wk, wv, wo = (sb(n, [P, KC, C]) for n in ("wq", "wk", "wv", "wo"))
        stage = sb("weights_in", [P, 2, CH])
        bqk_s = sb("bias_qk", [P, 2 * KC])
        bv_bc, bo_bc = sb("bias_v", [P, C]), sb("bias_o", [P, C])
        b1_s = sb("bias_1", [P, E * MC])
        wr32 = sb("router_in", [P, KC, E])
        wr = sb("router", [P, 2, KC, E], fp16)
        id32, id16 = sb("ident32", [P, P]), sb("ident16", [P, P], fp16)
        tri, ones = sb("strict_tri", [P, P], bf16), sb("ones", [P, P], bf16)
        tok = sb("token", [P, TOK // P], i32)
        expert_no = sb("expert_no", [P, E])
        region = sb("region_start", [P, E])
        base = sb("next_row", [P, E])
        mx = sb("maxima", [P, 2 * JT * (H // 2)])
        mrow = sb("minus_max_rows", [2 * JT * (H // 2), P], fp16)
        minus_half = sb("minus_half", [P, JT])
        stats = sb("stats", [P, JT, 6])
        mv = sb("mean_var", [P, JT, 2])
        rstd = sb("rstd", [P, JT])
        stats2 = sb("stats2", [P, JT, 6])
        mv2 = sb("mean_var2", [P, JT, 2])
        rstd2 = sb("rstd2", [P, JT])
        rsum = sb("one_by_sum", [P, JT, 4])
        lg = sb("logits", [P, JT, E])
        top = sb("top_logits", [P, JT, 8])
        topi = sb("top_index", [P, JT, 8], u32)
        topf = sb("top_index_f", [P, JT, 2])
        hot = sb("one_hot", [P, JT, 2, E])
        both = sb("both_hot", [P, JT, E], bf16)
        gap = sb("logit_gap", [P, JT])
        eg = sb("exp_gap", [P, JT])
        den = sb("denominator", [P, JT])
        wt = sb("pair_weight", [P, JT, 2])
        hw = sb("hot_weight", [P, JT, 2, E])
        pos8 = sb("rank_row", [P, JT, E])
        hp = sb("hot_row", [P, JT, 2, E])
        posf = sb("pair_row_f", [P, JT * 2])
        pos = sb("pair_row", [P, JT * 2], u32)
        tn, tni = sb("tiles_f", [1, E]), sb("tiles_i", [1, 2, E], i32)
        tcum = sb("tiles_cum", [1, E])
        one8 = sb("one8", [1, E])
        tix = sb("tile_no", [1, NT])
        tle, tlx = (area[0:1, VAT + i * NT * E:VAT + (i + 1) * NT * E].rearrange("p (t e) -> p t e", e=E)
                    for i in range(2))
        tex, trow = sb("tile_expert_f", [1, NT]), sb("tile_row_f", [1, NT])
        tskip = sb("tile_skip", [1, NT])
        te_i, tr_i = sb("tile_expert", [1, NT], i32), sb("tile_row", [1, NT], i32)
        pad_at = sb("pad_start", [1, E], i32)

        bank = [ctx.enter_context(nc.psum_tensor(f"bank{i}", [P, 512], fp32)) for i in range(8)]
        S_b = [bank[i][:, :].rearrange("p (j n) -> p j n", j=JT) for i in (0, 1)]
        T_b = [bank[i][:, :].rearrange("p (j n) -> p j n", j=JT) for i in (2, 3)]
        O_b = [bank[i][:, 0:JT * 4 * OW].rearrange("p (j h d) -> p j h d", j=JT, h=4) for i in (4, 5)]
        J_b = [bank[6], bank[7]]

        def semaphore(name):
            return ctx.enter_context(nc.semaphore(name))

        s_acc_pad_out, s_b1_in, s_b2_in, s_base_set, s_bo_in, s_both_hot, s_bqk_in, s_bv_in = (
            semaphore(n) for n in ("acc_pad_out", "b1_in", "b2_in", "base_set", "bo_in", "both_hot", "bqk_in", "bv_in"))
        s_const_set, s_consts, s_ctx_in, s_down_mm, s_exp_done, s_exp_gap, s_gap, s_gelu_done = (
            semaphore(n) for n in ("const_set", "consts", "ctx_in", "down_mm", "exp_done", "exp_gap", "gap", "gelu_done"))
        s_h_high, s_h_split, s_iotas, s_k_back, s_k_mm, s_k_out, s_k_read, s_k_split = (
            semaphore(n) for n in ("h_high", "h_split", "iotas", "k_back", "k_mm", "k_out", "k_read", "k_split"))
        s_ln1_steps, s_ln2_steps, s_logit_mm, s_logit_read, s_maxT_mm, s_maxT_read, s_max_done, s_max_row_in = (
            semaphore(n) for n in ("ln1_steps", "ln2_steps", "logit_mm", "logit_read", "maxT_mm", "maxT_read", "max_done", "max_row_in"))
        s_meta_in, s_oT_mm, s_oT_read, s_o_read, s_out, s_p_low, s_pad_made, s_pad_out = (
            semaphore(n) for n in ("meta_in", "oT_mm", "oT_read", "o_read", "out", "p_low", "pad_made", "pad_out"))
        s_pad_zero, s_pair_rows, s_pair_weight, s_pos_f, s_pv_mm, s_q_back, s_q_mm, s_q_out = (
            semaphore(n) for n in ("pad_zero", "pair_rows", "pair_weight", "pos_f", "pv_mm", "q_back", "q_mm", "q_out"))
        s_q_read, s_q_split, s_q_zero_out, s_qkv_const, s_qv_zero, s_rank_mm, s_rank_read, s_route_steps = (
            semaphore(n) for n in ("q_read", "q_split", "q_zero_out", "qkv_const", "qv_zero", "rank_mm", "rank_read", "route_steps"))
        s_router_split, s_rowT_mm, s_rowT_read, s_row_parts, s_rows_in, s_rstd, s_rstd2, s_rstd2_base = (
            semaphore(n) for n in ("router_split", "rowT_mm", "rowT_read", "row_parts", "rows_in", "rstd", "rstd2", "rstd2_base"))
        s_rstd_base, s_s_mm, s_scattered, s_st_mm, s_summed, s_sums_inverted, s_table, s_table_const = (
            semaphore(n) for n in ("rstd_base", "s_mm", "scattered", "st_mm", "summed", "sums_inverted", "table", "table_const"))
        s_table_steps, s_tile_T_mm, s_tile_T_read, s_up_mm, s_v_high, s_v_mm, s_v_read, s_v_split = (
            semaphore(n) for n in ("table_steps", "tile_T_mm", "tile_T_read", "up_mm", "v_high", "v_mm", "v_read", "v_split"))
        s_w_high, s_w_low, s_wk_in, s_wo_in, s_wq_in, s_wr_in, s_wv_in, s_x1_mm = (
            semaphore(n) for n in ("w_high", "w_low", "wk_in", "wo_in", "wq_in", "wr_in", "wv_in", "x1_mm"))
        s_x1_out, s_x1_read, s_xT_mm, s_xT_read, s_x_in, s_x_res_bias, s_x_res_in, s_xn_done = (
            semaphore(n) for n in ("x1_out", "x1_read", "xT_mm", "xT_read", "x_in", "x_res_bias", "x_res_in", "xn_done"))
        s_y_read, s_y_weighted = (
            semaphore(n) for n in ("y_read", "y_weighted"))
        s_w_in = [semaphore(f"w_in{i}") for i in range(2)]

        def due(value):
            return not isinstance(value, int) or value > 0

        def apart(eng, value):
            if isinstance(value, int):
                return value
            held = eng.to_reg(value)
            eng.wait_ge(s_iotas, 4)
            return held

        uses = [("k", 0, 0, s_k_read), ("v", 1, 0, s_v_read), ("oT", 0, 3, s_oT_read), ("xT", 1, 0, s_xT_read),
                ("q", 0, 0, s_q_read), ("x1", 1, 3, s_x1_read), ("rowT", 0, 3, s_rowT_read),
                ("logit", 1, 3, s_logit_read), ("rank", 0, 3, s_rank_read), ("maxT", 1, 1, s_maxT_read)]

        def bank_of(name):
            return next(u[1] for u in uses if u[0] == name)

        def bank_user_before(name, t, static):
            at = next(i for i, u in enumerate(uses) if u[0] == name)
            step, i = 0, at
            while True:
                i -= 1
                if i < 0:
                    i, step = len(uses) - 1, step + 1
                _, bank_no, stage, read = uses[i]
                if static and t - step < 0:
                    return None
                if bank_no == uses[at][1] and (not static or 0 <= t - step - stage < B):
                    return read, t - step - stage + 1

        def stages(t, static):
            return [t - s if not static or 0 <= t - s < B else None for s in range(4)]

        def pipeline(eng, step):
            for t in range(4):
                step(t, True)
            with eng.Fori(4, B) as t:
                step(t, False)
            for t in range(B, STEPS):
                step(t, True)

        def expert_of(t, static):
            return t - 2 if not static or 0 <= t - 2 < PRE else None

        block = ctx.enter_context(nc.Block())

        @block.sync
        def _(sp):
            def load_x(b):
                sp.dma_start(x_in[:, :, :],
                             x[ds(b * N, N), :].rearrange("(j p) c -> p j c", p=P)).then_inc(s_x_in, 16)

            def load_ctx(b):
                sp.dma_start(ctx_T,
                             ctxT[ds(b, 1), :, :].rearrange("b (k p) n -> p (b k) n", p=P)).then_inc(s_ctx_in, 16)

            load_x(0)
            load_ctx(0)
            sp.dma_start(wk[:, :, :], wkT.rearrange("(k p) c -> p k c", p=P)).then_inc(s_wk_in, 16)
            sp.dma_start(bqk_s[:, :], bqk).then_inc(s_bqk_in, 16)
            sp.dma_start(wv[:, :, :], wvT.rearrange("(k p) c -> p k c", p=P)).then_inc(s_wv_in, 16)
            sp.dma_start(bv_bc[:, :], bv.partition_broadcast(P)).then_inc(s_bv_in, 16)
            sp.dma_start(wq[:, :, :], wqT.rearrange("(k p) c -> p k c", p=P)).then_inc(s_wq_in, 16)
            sp.dma_start(wo[:, :, :], woT.rearrange("(k p) c -> p k c", p=P)).then_inc(s_wo_in, 16)
            sp.dma_start(bo_bc[:, :], bo.partition_broadcast(P)).then_inc(s_bo_in, 16)
            sp.dma_start(wr32[:, :, :], wrT.rearrange("(k p) e -> p k e", p=P)).then_inc(s_wr_in, 16)
            sp.dma_start(b1_s[:, :], b1).then_inc(s_b1_in, 16)
            sp.wait_ge(s_pad_made, 2)
            sp.dma_start(q_st[:, :, R3, :].rearrange("b h n -> (b h) n"),
                         pad[:, 0:N // 2].bitcast(fp16)).then_inc(s_q_zero_out, 16)
            sp.dma_start(routed[E * REG:E * REG + P, :], pad[:, :]).then_inc(s_pad_out, 16)
            sp.dma_start(acc[TOK:TOK + P, :], pad[:, 0:C]).then_inc(s_acc_pad_out, 16)

            def load_weights(e, c):
                n = NCH * e + c
                if due(n - 1):
                    sp.wait_ge(s_w_high, apart(sp, n - 1))
                if due(n - 1):
                    sp.wait_ge(s_w_low, apart(sp, n - 1))
                sp.dma_start(stage[:, c % 2, :],
                             w12[ds(e, 1), :, c * CH:(c + 1) * CH].rearrange("e p w -> (e p) w")).then_inc(s_w_in[c % 2], 16)

            def step(t, static):
                b_a, b_s, b_c, b_d = stages(t, static)
                e = expert_of(t, static)
                if b_a is not None and (not static or b_a > 0):
                    if due(2 * b_a):
                        sp.wait_ge(s_xn_done, apart(sp, 2 * b_a))
                    load_x(b_a)
                    if due(b_a):
                        sp.wait_ge(s_v_mm, apart(sp, b_a))
                    load_ctx(b_a)
                if e is not None:
                    load_weights(e, 0)
                    load_weights(e, 1)
                if b_d is not None:
                    if due(b_d):
                        sp.wait_ge(s_x1_read, apart(sp, b_d))
                    sp.dma_start(x_res[:, :, :],
                                 x[ds(b_d * N, N), :].rearrange("(j p) c -> p j c", p=P)).then_inc(s_x_res_in, 16)
                if b_a is not None:
                    sp.wait_ge(s_k_split, apart(sp, b_a + 1))
                    for r, part in enumerate((0, 1, 0)):
                        for c in range(KC):
                            sp.dma_start(k_st[ds(b_a, 1), c * 8:c * 8 + 8, r * D:(r + 1) * D, :].rearrange( "b h d n -> (b h) d n"),
                                         k16[:, part, c, :]).then_inc(s_k_out, 16)
                    sp.wait_ge(s_k_out, apart(sp, 96 * (b_a + 1)))
                    if due(16 * b_a):
                        sp.wait_ge(s_k_back, apart(sp, 16 * b_a))
                    if due(H * (b_a - 2)):
                        sp.wait_ge(s_st_mm, apart(sp, H * (b_a - 2)))
                    sp.wait_ge(s_qkv_const, 4)
                    src = k_st[ds(b_a, 1), :, 0:R3, :].rearrange("b (h s) r n -> s r (b h) n", s=2)
                    for s in range(2):
                        sp.dma_start(Ks[s * HR:s * HR + R3, ds(b_a % 3, 1), :, :].rearrange("p r h n -> p (r h) n"),
                                     src[s]).then_inc(s_k_back, 16)
                if e is not None:
                    load_weights(e, 2)
                if b_a is not None:
                    sp.wait_ge(s_q_split, apart(sp, b_a + 1))
                    for r, part in enumerate((0, 0, 1)):
                        for c in range(KC):
                            sp.dma_start(q_st[ds(b_a, 1), c * 8:c * 8 + 8, r * D:(r + 1) * D, :].rearrange( "b h d n -> (b h) d n"),
                                         q16[:, part, c, :]).then_inc(s_q_out, 16)
                    sp.wait_ge(s_q_out, apart(sp, 96 * (b_a + 1)))
                    sp.wait_ge(s_q_zero_out, 16)
                    if due(32 * b_a):
                        sp.wait_ge(s_q_back, apart(sp, 32 * b_a))
                    src = q_st[ds(b_a, 1), :, 0:R3 + 1, :].rearrange("b (h s) r n -> s r (b h) n", s=2)
                    for s in range(2):
                        sp.dma_start(Qs[s * HR:s * HR + R3 + 1, ds(b_a % 3, 1), s::2, :].rearrange("p r h n -> p (r h) n"),
                                     src[s]).then_inc(s_q_back, 16)
                if b_d is not None:
                    sp.wait_ge(s_x1_read, apart(sp, b_d + 1))
                    sp.dma_start(acc[ds(b_d * N, N), :].rearrange("(j p) c -> p j c", p=P),
                                 x1[:, :, :]).then_inc(s_x1_out, 16)
                if e is not None:
                    load_weights(e, 3)

            pipeline(sp, step)
            sp.wait_ge(s_pv_mm, H * B)
            sp.dma_start(b2_bc,
                         b2.rearrange("(o e) c -> o (e c)", o=1)[0].partition_broadcast(P).rearrange( "p (e c) -> p e c", e=E)).then_inc(s_b2_in, 16)
            for e in range(PRE, E):
                for c in range(NCH):
                    load_weights(e, c)
            sp.wait_ge(s_table, 3)
            sp.wait_ge(s_pad_out, 16)
            for e in range(E):
                at = sp.value_load(pad_at[0:1, e:e + 1], min_val=0, max_val=E * REG - P)
                sp.dma_start(routed[ds(at, P), :], pad[:, :]).then_inc(s_pad_out, 16)
            sp.wait_ge(s_pad_out, 16 * (E + 1))
            sp.wait_ge(s_scattered, 64 * B)

            def rows_in(t, p):
                at = sp.value_load(tr_i[0:1, ds(t, 1)], min_val=0, max_val=E * REG)
                if due(t - 1):
                    sp.wait_ge(s_tile_T_mm, apart(sp, t - 1))
                if due(16 * t):
                    sp.wait_ge(s_rows_in, apart(sp, 16 * t))
                sp.dma_start(xr[:, p, :], routed[ds(at, P), 0:C]).then_inc(s_rows_in, 16)

            def meta_in(t, p):
                at = sp.value_load(tr_i[0:1, ds(t, 1)], min_val=0, max_val=E * REG)
                if due(16 * (t - 1)):
                    sp.wait_ge(s_summed, apart(sp, 16 * (t - 1)))
                if due(16 * t):
                    sp.wait_ge(s_meta_in, apart(sp, 16 * t))
                sp.dma_start(meta[:, p, 0:E + 1], routed[ds(at, P), R_ID:R_ID + E + 1]).then_inc(s_meta_in, 16)

            rows_in(0, 0)
            rows_in(1, 1)
            meta_in(0, 0)
            rows_in(2, 0)
            meta_in(1, 1)
            with sp.Fori(3, NT - 1, 2) as t:
                rows_in(t, 1)
                meta_in(t - 1, 0)
                rows_in(t + 1, 0)
                meta_in(t, 1)
            meta_in(NT - 1, 0)
            sp.wait_ge(s_summed, 16 * NT)
            sp.dma_start(out.rearrange("b n c -> (b n) c"), acc[0:TOK, :]).then_inc(s_out, 16)
            sp.wait_ge(s_out, 16)

        @block.tensor
        def _(pe):
            mm = nc.tensor.matmul

            def attend_scores(b, h):
                if h == 0:
                    pe.wait_ge(s_k_back, 32 * (b + 1))
                    pe.wait_ge(s_q_back, 32 * (b + 1))
                if due(H * b + h - 1):
                    pe.wait_ge(s_max_done, H * b + h - 1)
                for j in range(JT):
                    last = mm(S_b[h % 2][:, j, :], Qs[:, ds(b % 3, 1), h, j * P:(j + 1) * P],
                              Ks[:, ds(b % 3, 1), h // 2, :], start=True, stop=True)
                last.then_inc(s_s_mm, 1)

            def attend_scores_T(b, h):
                if h == 0:
                    pe.wait_ge(s_max_row_in, 64 * (b + 1))
                if due(H * b + h - 1):
                    pe.wait_ge(s_exp_done, H * b + h - 1)
                for j in range(JT):
                    last = mm(T_b[h % 2][:, j, :], Ks[:, ds(b % 3, 1), h // 2, j * P:(j + 1) * P],
                              Qs[:, ds(b % 3, 1), h, :], start=True, stop=True)
                last.then_inc(s_st_mm, 1)

            def attend_values(b, h):
                if h % 4 == 0:
                    if due(4 * b + h // 4 - 1):
                        pe.wait_ge(s_o_read, 4 * b + h // 4 - 1)
                if h == 0:
                    pe.wait_ge(s_v_split, b + 1)
                    pe.wait_ge(s_v_high, b + 1)
                pe.wait_ge(s_p_low, H * b + h + 1)
                ph = Pe[:, h % 4, :, :].bitcast(bf16)
                for j in range(JT):
                    o = O_b[(h // 4) % 2][:, j, h % 4, :]
                    for k in range(JT):
                        hi = ph[:, k, 2 * j * P + 1:2 * (j + 1) * P:2]
                        mm(o, hi, Vh[:, ds(b % 3, 1), k, h, 0:OW], start=k == 0, stop=False)
                        mm(o, hi, Vl[:, ds(b % 3, 1), k, h, 0:OW], start=False, stop=False)
                        last = mm(o, Pl[:, h % 4, k, j * P:(j + 1) * P], Vh[:, ds(b % 3, 1), k, h, 0:OW],
                                  start=False, stop=k == JT - 1)
                last.then_inc(s_pv_mm, 1)

            def project_T(name, w, src, made, t, static):
                if before := bank_user_before(name, t, static):
                    pe.wait_ge(*before)
                ps = J_b[bank_of(name)][:, :].rearrange("p (c n) -> p c n", c=KC)
                for c in range(KC):
                    for k in range(KC):
                        last = mm(ps[:, c, :], w[:, k, c * P:(c + 1) * P], src[:, k, :], start=k == 0, stop=k == KC - 1)
                last.then_inc(made, 1)

            def project(name, w, src, made, t, static):
                if before := bank_user_before(name, t, static):
                    pe.wait_ge(*before)
                ps = J_b[bank_of(name)][:, :].rearrange("p (j c) -> p j c", j=JT)
                for j in range(JT):
                    for k in range(KC):
                        last = mm(ps[:, j, :], src[:, k, j * P:(j + 1) * P], w[:, k, :], start=k == 0, stop=k == KC - 1)
                last.then_inc(made, 1)

            def transposed(name, src, made, t, static):
                if before := bank_user_before(name, t, static):
                    pe.wait_ge(*before)
                ps = J_b[bank_of(name)][:, :].rearrange("p (k n) -> p k n", k=KC)
                for k in range(KC):
                    for j in range(JT):
                        last = nc.tensor.transpose(ps[:, k, j * P:(j + 1) * P], src[:, j, k * P:(k + 1) * P], id32[:, :])
                last.then_inc(made, 1)

            def step(t, static):
                b_a, b_s, b_c, b_d = stages(t, static)
                for i in range(SLOTS):
                    if b_a is not None:
                        if i == 0:
                            pe.wait_ge(s_ctx_in, 16 * (b_a + 1))
                            pe.wait_ge(s_wk_in, 16)
                            project_T("k", wk, ctx_T, s_k_mm, t, static)
                        if i == 1:
                            pe.wait_ge(s_wv_in, 16)
                            project("v", wv, ctx_T, s_v_mm, t, static)
                    if b_d is not None and i == 2:
                        pe.wait_ge(s_o_read, 4 * (b_d + 1))
                        transposed("oT", o_n, s_oT_mm, t, static)
                    if b_a is not None:
                        if i == 3:
                            pe.wait_ge(s_xn_done, 2 * (b_a + 1))
                            pe.wait_ge(s_consts, 4)
                            transposed("xT", xn, s_xT_mm, t, static)
                        if i == 5:
                            pe.wait_ge(s_xT_read, b_a + 1)
                            pe.wait_ge(s_wq_in, 16)
                            project_T("q", wq, xnT, s_q_mm, t, static)
                    if b_d is not None:
                        if i == 6:
                            pe.wait_ge(s_oT_read, b_d + 1)
                            pe.wait_ge(s_wo_in, 16)
                            project("x1", wo, oT, s_x1_mm, t, static)
                        if i == 10:
                            if before := bank_user_before("rowT", t, static):
                                pe.wait_ge(*before)
                            pe.wait_ge(s_row_parts, b_d + 1)
                            ps = J_b[bank_of("rowT")][:, :].bitcast(fp16).rearrange("p (j s n) -> p j s n", j=JT, s=4)
                            for j in range(JT):
                                for s in range(2 * KC):
                                    last = nc.tensor.transpose(ps[:, j, s, :], rows16[:, j, s * P:(s + 1) * P], id16[:, :])
                            last.then_inc(s_rowT_mm, 1)
                        if i == 12:
                            if before := bank_user_before("logit", t, static):
                                pe.wait_ge(*before)
                            pe.wait_ge(s_rowT_read, b_d + 1)
                            pe.wait_ge(s_router_split, 2)
                            for j in range(JT):
                                ps = J_b[bank_of("logit")][:, j * E:(j + 1) * E]
                                for k in range(KC):
                                    mm(ps, xt2[:, j, k, :], wr[:, 0, k, :], start=k == 0, stop=False)
                                    mm(ps, xt2[:, j, k, :], wr[:, 1, k, :], start=False, stop=False)
                                    last = mm(ps, xt2[:, j, KC + k, :], wr[:, 0, k, :], start=False, stop=k == KC - 1)
                            last.then_inc(s_logit_mm, 1)
                        if i == 15:
                            if before := bank_user_before("rank", t, static):
                                pe.wait_ge(*before)
                            pe.wait_ge(s_both_hot, b_d + 1)
                            ps = J_b[bank_of("rank")]
                            mm(ps[:, 0:E], tri[:, :], both[:, 0, :], start=True, stop=True)
                            mm(ps[:, E:2 * E], tri[:, :], both[:, 1, :], start=True, stop=False)
                            mm(ps[:, E:2 * E], ones[:, :], both[:, 0, :], start=False, stop=True)
                            mm(ps[:, 2 * E:3 * E], ones[:, :], both[:, 0, :], start=True, stop=False)
                            mm(ps[:, 2 * E:3 * E], ones[:, :], both[:, 1, :], start=False, stop=True).then_inc(
                                s_rank_mm, 1)
                    if b_s is not None:
                        if i < H:
                            attend_scores(b_s, i)
                        if i == H + 2:
                            if before := bank_user_before("maxT", t, static):
                                pe.wait_ge(*before)
                            pe.wait_ge(s_max_done, H * (b_s + 1))
                            nc.tensor.transpose(J_b[bank_of("maxT")][0:32, 0:P], mx[:, :], id32[:, :]).then_inc(
                                s_maxT_mm, 1)
                    if b_c is not None:
                        if LAG_ST <= i < H + LAG_ST:
                            attend_scores_T(b_c, i - LAG_ST)
                        if i >= LAG_PV:
                            attend_values(b_c, i - LAG_PV)

            pipeline(pe, step)

            def tile_T(t, p):
                pe.wait_ge(s_rows_in, 16 * (t + 1))
                if due(t):
                    pe.wait_ge(s_tile_T_read, t)
                ps = bank[6][:, 0:2 * P].bitcast(fp16).rearrange("p (s n) -> p s n", s=2 * KC)
                src = xr[:, p, :].bitcast(fp16)
                for s in range(2 * KC):
                    last = nc.tensor.transpose(ps[:, s, :], src[:, s * P:(s + 1) * P], id16[:, :])
                last.then_inc(s_tile_T_mm, 1)

            def up(t, p):
                e = pe.value_load(te_i[0:1, ds(t, 1)], min_val=0, max_val=E - 1)
                pe.wait_ge(s_tile_T_read, t + 1)
                for m in range(MC):
                    if m % 4 == 0:
                        if due(MC * (t - 2) + m + 4):
                            pe.wait_ge(s_gelu_done, MC * (t - 2) + m + 4)
                    ps = bank[2 * p + m // 4][:, (m % 4) * P:(m % 4 + 1) * P]
                    for k in range(KC):
                        at = k * M + m * P
                        hi, lo = Wx[:, ds(e, 1), at:at + P], Wx[:, ds(e, 1), EH + at:EH + at + P]
                        mm(ps, hi, xT[:, p, k, :], start=k == 0, stop=False)
                        mm(ps, hi, xT[:, p, KC + k, :], start=False, stop=False)
                        last = mm(ps, lo, xT[:, p, k, :], start=False, stop=k == KC - 1)
                    if m % 4 == 3:
                        last.then_inc(s_up_mm, 1)

            def down(t, p):
                e = pe.value_load(te_i[0:1, ds(t, 1)], min_val=0, max_val=E - 1)
                if due(t - 1):
                    pe.wait_ge(s_y_read, t - 1)
                ps = bank[4 + p][:, 0:C]
                for m in range(MC):
                    if m % 4 == 0:
                        pe.wait_ge(s_h_split, 2 * t + m // 4 + 1)
                    at = KC * M + m * C
                    hi, lo = Wx[:, ds(e, 1), at:at + C], Wx[:, ds(e, 1), EH + at:EH + at + C]
                    mm(ps, hh[:, p, m, :], hi, start=m == 0, stop=False)
                    mm(ps, hh[:, p, m, :], lo, start=False, stop=False)
                    last = mm(ps, hl[:, p, m, :], hi, start=False, stop=m == MC - 1)
                last.then_inc(s_down_mm, 1)

            pe.wait_ge(s_table, 3)
            pe.wait_ge(s_w_high, NCH * E)
            pe.wait_ge(s_w_low, NCH * E)
            tile_T(0, 0)
            up(0, 0)
            tile_T(1, 1)
            up(1, 1)
            tile_T(2, 0)
            down(0, 0)
            up(2, 0)
            tile_T(3, 1)
            down(1, 1)
            with pe.Fori(3, NT - 2, 2) as t:
                up(t, 1)
                tile_T(t + 1, 0)
                down(t - 1, 0)
                up(t + 1, 0)
                tile_T(t + 2, 1)
                down(t, 1)
            up(NT - 2, 1)
            tile_T(NT - 1, 0)
            down(NT - 3, 0)
            up(NT - 1, 0)
            down(NT - 2, 1)
            down(NT - 1, 0)

        @block.scalar
        def _(act):
            A = nc.scalar.activation

            def heads_T(name, dst, first):
                ps = J_b[bank_of(name)][:, :].rearrange("p (c n) -> p c n", c=KC)
                for c in range(KC):
                    bias = bqk_s[:, first + c:first + c + 1]
                    A(qk32[:, c, :], ps[:, c, :], ACT.Identity, bias=bias)
                    last = A(dst[:, 0, c, :], ps[:, c, :], ACT.Identity, bias=bias)
                return last

            def w_high(e, c):
                n = NCH * e + c
                act.wait_ge(s_w_in[c % 2], 32 * e + 16 * (c // 2 + 1))
                A(Wx[:, ds(e, 1), c * CH:(c + 1) * CH], stage[:, c % 2, :], ACT.Copy, scale=WS).then_inc(s_w_high, 1)

            def step(t, static):
                b_a, b_s, b_c, b_d = stages(t, static)
                e = expert_of(t, static)
                for i in range(SLOTS):
                    if b_a is not None:
                        if i == 0:
                            act.wait_ge(s_k_mm, b_a + 1)
                            act.wait_ge(s_bqk_in, 16)
                            if due(b_a):
                                act.wait_ge(s_q_split, b_a)
                                act.wait_ge(s_k_out, 96 * b_a)
                            heads_T("k", k16, KC).then_inc(s_k_read, 1)
                        if i == 5:
                            act.wait_ge(s_q_mm, b_a + 1)
                            act.wait_ge(s_k_split, b_a + 1)
                            if due(b_a):
                                act.wait_ge(s_q_out, 96 * b_a)
                            heads_T("q", q16, 0).then_inc(s_q_read, 1)
                        if i == 2:
                            act.wait_ge(s_v_read, b_a + 1)
                            if due(H * (b_a - 2)):
                                act.wait_ge(s_pv_mm, H * (b_a - 2))
                            act.wait_ge(s_qkv_const, 4)
                            A(Vh[:, ds(b_a % 3, 1), :, :, 0:D].rearrange("p r j h d -> p (r j) h d"),
                              v32.rearrange("p j (h d) -> p j h d", h=H), ACT.Copy).then_inc(s_v_high, 1)
                        if i == 4:
                            act.wait_ge(s_xT_mm, b_a + 1)
                            if due(b_a):
                                act.wait_ge(s_q_mm, b_a)
                            A(xnT, J_b[bank_of("xT")][:, :].rearrange("p (k n) -> p k n", k=KC), ACT.Copy).then_inc(
                                s_xT_read, 1)
                    if b_d is not None:
                        if i == 3:
                            act.wait_ge(s_oT_mm, b_d + 1)
                            if due(b_d):
                                act.wait_ge(s_x1_mm, b_d)
                            A(oT, J_b[bank_of("oT")][:, :].rearrange("p (k n) -> p k n", k=KC), ACT.Copy).then_inc(
                                s_oT_read, 1)
                        if i == 11:
                            act.wait_ge(s_rowT_mm, b_d + 1)
                            if due(b_d):
                                act.wait_ge(s_logit_mm, b_d)
                            ps = J_b[bank_of("rowT")][:, :].bitcast(fp16).rearrange("p (j s n) -> p j s n", j=JT, s=4)
                            A(xt2[:, :, :, :], ps, ACT.Copy).then_inc(s_rowT_read, 1)
                        if i == 14:
                            act.wait_ge(s_gap, b_d + 1)
                            if due(b_d):
                                act.wait_ge(s_pair_weight, b_d)
                            A(eg[:, :], gap[:, :], ACT.Exp).then_inc(s_exp_gap, 1)
                    if b_c is not None and LAG_ST <= i < H + LAG_ST:
                        h = i - LAG_ST
                        act.wait_ge(s_st_mm, H * b_c + h + 1)
                        if due(H * b_c + h - 3):
                            act.wait_ge(s_pv_mm, H * b_c + h - 3)
                        A(Pe[:, h % 4, :, :], T_b[h % 2], ACT.Exp, scale=float(D) ** -0.5).then_inc(s_exp_done, 1)
                    if e is not None and i in (6, 9, 12, 16):
                        w_high(e, (6, 9, 12, 16).index(i))
                    if b_s is not None and i == H + 2:
                        act.wait_ge(s_maxT_mm, b_s + 1)
                        if due(64 * b_s):
                            act.wait_ge(s_max_row_in, 64 * b_s)
                        A(mrow[:, :], J_b[bank_of("maxT")][0:32, 0:P], ACT.Copy, scale=-1.0).then_inc(s_maxT_read, 1)
                        act.wait_ge(s_maxT_read, b_s + 1)
                        for s in range(2):
                            for j in range(JT):
                                at = (s * JT + j) * (H // 2)
                                act.dma_start(Qs[s * HR + R3:s * HR + R3 + 1, ds(b_s % 3, 1), s::2,
                                                 j * P:(j + 1) * P].rearrange("p r h n -> p (r h) n"),
                                              mrow[at:at + H // 2, :]).then_inc(s_max_row_in, 16)

            pipeline(act, step)
            act.wait_ge(s_pv_mm, H * B)
            for e in range(PRE, E):
                for c in range(NCH):
                    w_high(e, c)

            def copy_T(t, p):
                act.wait_ge(s_tile_T_mm, t + 1)
                if due(2 * (t - 1)):
                    act.wait_ge(s_up_mm, 2 * (t - 1))
                ps = bank[6][:, 0:2 * P].bitcast(fp16).rearrange("p (s n) -> p s n", s=2 * KC)
                A(xT[:, p, :, :], ps, ACT.Copy).then_inc(s_tile_T_read, 1)

            def gelu(t, p):
                e = act.value_load(te_i[0:1, ds(t, 1)], min_val=0, max_val=E - 1)
                for m in range(MC):
                    if m % 4 == 0:
                        if due(2 * (t - 2) + m // 4 + 1):
                            act.wait_ge(s_h_split, 2 * (t - 2) + m // 4 + 1)
                        act.wait_ge(s_up_mm, 2 * t + m // 4 + 1)
                    ps = bank[2 * p + m // 4][:, (m % 4) * P:(m % 4 + 1) * P]
                    A(h32[:, p, m, :], ps, ACT.Gelu, bias=b1_s[:, ds(e * MC + m, 1)], scale=1 / (XS * WS)).then_inc(
                        s_gelu_done, 1)

            act.wait_ge(s_table, 3)
            act.wait_ge(s_b1_in, 16)
            copy_T(0, 0)
            gelu(0, 0)
            copy_T(1, 1)
            gelu(1, 1)
            copy_T(2, 0)
            gelu(2, 0)
            copy_T(3, 1)
            with act.Fori(3, NT - 2, 2) as t:
                gelu(t, 1)
                copy_T(t + 1, 0)
                gelu(t + 1, 0)
                copy_T(t + 2, 1)
            gelu(NT - 2, 1)
            copy_T(NT - 1, 0)
            gelu(NT - 1, 0)

        @block.vector
        def _(dve):
            V = nc.vector

            V.memset(pad[:, :], 0.0).then_inc(s_pad_zero, 1)
            dve.wait_ge(s_pad_zero, 1)
            dve.wait_ge(s_iotas, 4)
            V.tensor_scalar(pad[:, R_ID:R_ID + 1].bitcast(i32), tok[:, 0:1], TOK, None, ALU.add).then_inc(s_pad_made, 2)
            V.memset(spare[:, 0:NQ + NV].bitcast(u32), 0).then_inc(s_qv_zero, 1)
            V.memset(spare[:, NQ + NV:NQ + 2 * NV].bitcast(u32), 0).then_inc(s_qkv_const, 1)
            V.memset(Ks, 1.0).then_inc(s_qkv_const, 1)
            dve.wait_ge(s_qv_zero, 1)
            V.memset(Vh[:, :, :, :, D:D + 1], 1.0).then_inc(s_qkv_const, 1)
            V.memset(rows[:, :, :], 0.0).then_inc(s_qkv_const, 1)
            V.memset(one8[:, :], 1.0).then_inc(s_table_const, 1)
            dve.wait_ge(s_wr_in, 16)
            V.tensor_scalar(wr[:, 0, :, :], wr32[:, :, :], WS, None, ALU.mult).then_inc(s_router_split, 1)
            dve.wait_ge(s_router_split, 1)
            V.scalar_tensor_tensor(out=wr[:, 1, :, :], in0=wr32[:, :, :], scalar=WS, in1=wr[:, 0, :, :],
                                   op0=ALU.mult, op1=ALU.subtract).then_inc(s_router_split, 1)

            def w_low(e, c):
                n = NCH * e + c
                dve.wait_ge(s_w_high, n + 1)
                at = c * CH
                V.scalar_tensor_tensor(out=Wx[:, ds(e, 1), EH + at:EH + at + CH].rearrange("p e w -> p (e w)"),
                                       in0=stage[:, c % 2, :], scalar=WS,
                                       in1=Wx[:, ds(e, 1), at:at + CH].rearrange("p e w -> p (e w)"),
                                       op0=ALU.mult, op1=ALU.subtract).then_inc(s_w_low, 1)

            def norm_stats(src, st, m, steps, before):
                for j in range(JT):
                    last = V.bn_stats(st[:, j, :], src[:, j, :])
                last.then_inc(steps, 1)
                dve.wait_ge(steps, apart(dve, before + 1))
                for j in range(JT):
                    last = V.bn_aggr(m[:, j, :], st[:, j, :])
                last.then_inc(steps, 1)

            def step(t, static):
                b_a, b_s, b_c, b_d = stages(t, static)
                e = expert_of(t, static)
                for i in range(SLOTS):
                    if b_a is not None:
                        if i == 0:
                            dve.wait_ge(s_x_in, 16 * (b_a + 1))
                            if due(2 * b_a):
                                dve.wait_ge(s_xn_done, 2 * b_a)
                            norm_stats(x_in, stats, mv, s_ln1_steps, 2 * b_a)
                        if i == 1:
                            dve.wait_ge(s_k_read, b_a + 1)
                            if due(96 * b_a):
                                dve.wait_ge(s_k_out, 96 * b_a)
                            V.tensor_tensor(k16[:, 1, :, :], qk32, k16[:, 0, :, :], ALU.subtract).then_inc(
                                s_k_split, 1)
                            dve.wait_ge(s_v_mm, b_a + 1)
                            dve.wait_ge(s_bv_in, 16)
                            if due(b_a):
                                dve.wait_ge(s_v_high, b_a)
                            if due(b_a):
                                dve.wait_ge(s_v_split, b_a)
                            V.tensor_tensor(v32, J_b[bank_of("v")][:, :].rearrange("p (j c) -> p j c", j=JT),
                                            bv_bc[:, :].unsqueeze(1).broadcast_to([P, JT, C]), ALU.add).then_inc(
                                s_v_read, 1)
                        if i == 2:
                            dve.wait_ge(s_rstd, b_a + 1)
                            if due(b_a):
                                dve.wait_ge(s_xT_mm, b_a)
                            for j in range(JT):
                                V.tensor_scalar(xn[:, j, :], x_in[:, j, :], mv[:, j, 0:1], rstd[:, j:j + 1],
                                                ALU.subtract, ALU.mult).then_inc(s_xn_done, 1)
                        if i == 3:
                            dve.wait_ge(s_v_high, b_a + 1)
                            dve.wait_ge(s_v_read, b_a + 1)
                            r = ds(b_a % 3, 1)
                            V.tensor_tensor(Vl[:, r, :, :, 0:D].rearrange("p r j h d -> p (r j) h d"),
                                            v32.rearrange("p j (h d) -> p j h d", h=H),
                                            Vh[:, r, :, :, 0:D].rearrange("p r j h d -> p (r j) h d"),
                                            ALU.subtract).then_inc(s_v_split, 1)
                        if i == 6:
                            dve.wait_ge(s_q_read, b_a + 1)
                            if due(96 * b_a):
                                dve.wait_ge(s_q_out, 96 * b_a)
                            V.tensor_tensor(q16[:, 1, :, :], qk32, q16[:, 0, :, :], ALU.subtract).then_inc(
                                s_q_split, 1)
                    if b_d is not None:
                        if i == 7:
                            dve.wait_ge(s_x1_mm, b_d + 1)
                            dve.wait_ge(s_x_res_bias, b_d + 1)
                            if due(16 * b_d):
                                dve.wait_ge(s_x1_out, 16 * b_d)
                            if due(LN2 * b_d):
                                dve.wait_ge(s_ln2_steps, LN2 * b_d)
                            V.tensor_tensor(x1[:, :, :], J_b[bank_of("x1")][:, :].rearrange("p (j c) -> p j c", j=JT),
                                            x_res[:, :, :], ALU.add).then_inc(s_x1_read, 1)
                            dve.wait_ge(s_x1_read, b_d + 1)
                            norm_stats(x1, stats2, mv2, s_ln2_steps, LN2 * b_d)
                        if i == 9:
                            dve.wait_ge(s_rstd2, b_d + 1)
                            if due(b_d):
                                dve.wait_ge(s_row_parts, b_d)
                            for j in range(JT):
                                V.tensor_scalar(xn2[:, j, :], x1[:, j, :], mv2[:, j, 0:1], rstd2[:, j:j + 1],
                                                ALU.subtract, ALU.mult).then_inc(s_ln2_steps, 1)
                            dve.wait_ge(s_ln2_steps, LN2 * b_d + 4)
                            if due(64 * b_d):
                                dve.wait_ge(s_scattered, 64 * b_d)
                            dve.wait_ge(s_qkv_const, 4)
                            V.tensor_scalar(rows16[:, :, 0:C], xn2[:, :, :], XS, None, ALU.mult).then_inc(
                                s_ln2_steps, 1)
                            dve.wait_ge(s_ln2_steps, LN2 * b_d + 5)
                            V.scalar_tensor_tensor(out=rows16[:, :, C:2 * C], in0=xn2[:, :, :], scalar=XS,
                                                   in1=rows16[:, :, 0:C], op0=ALU.mult, op1=ALU.subtract).then_inc(
                                s_row_parts, 1)
                        if i == 13:
                            dve.wait_ge(s_logit_mm, b_d + 1)
                            V.tensor_scalar(lg[:, :, :], J_b[bank_of("logit")][:, 0:JT * E].rearrange(
                                "p (j e) -> p j e", j=JT), 1 / (XS * WS), None, ALU.mult).then_inc(s_logit_read, 1)
                            dve.wait_ge(s_logit_read, apart(dve, b_d + 1))
                            for j in range(JT):
                                last = V.max(top[:, j, :], lg[:, j, :])
                            last.then_inc(s_route_steps, 1)
                            dve.wait_ge(s_route_steps, apart(dve, ROUTE * b_d + 1))
                            for j in range(JT):
                                last = V.max_index(topi[:, j, :], top[:, j, :], lg[:, j, :])
                            last.then_inc(s_route_steps, 1)
                            if due(b_d):
                                dve.wait_ge(s_exp_gap, b_d)
                            V.tensor_tensor(gap[:, :], top[:, :, 1], top[:, :, 0], ALU.subtract).then_inc(s_gap, 1)
                            dve.wait_ge(s_route_steps, ROUTE * b_d + 2)
                            V.tensor_copy(topf[:, :, :], topi[:, :, 0:2]).then_inc(s_route_steps, 1)
                            dve.wait_ge(s_route_steps, ROUTE * b_d + 3)
                            V.tensor_tensor(
                                hot[:, :, :, :], expert_no[:, :].unsqueeze(1).unsqueeze(1).broadcast_to([P, JT, 2, E]),
                                topf[:, :, :].unsqueeze(3).broadcast_to([P, JT, 2, E]), ALU.is_equal).then_inc(s_route_steps, 1)
                            dve.wait_ge(s_route_steps, ROUTE * b_d + 4)
                            if due(b_d):
                                dve.wait_ge(s_rank_mm, b_d)
                            V.tensor_tensor(both[:, :, :], hot[:, :, 0, :], hot[:, :, 1, :], ALU.add).then_inc(
                                s_both_hot, 1)
                        if i == 15:
                            dve.wait_ge(s_exp_gap, b_d + 1)
                            V.tensor_scalar(den[:, :], eg[:, :], 1.0, None, ALU.add).then_inc(s_route_steps, 1)
                            dve.wait_ge(s_route_steps, ROUTE * b_d + 5)
                            V.reciprocal(wt[:, :, 0], den[:, :]).then_inc(s_route_steps, 1)
                            dve.wait_ge(s_route_steps, ROUTE * b_d + 6)
                            V.tensor_tensor(wt[:, :, 1], wt[:, :, 0], eg[:, :], ALU.mult).then_inc(s_pair_weight, 1)
                            dve.wait_ge(s_pair_weight, b_d + 1)
                            V.tensor_tensor(hw[:, :, :, :], hot[:, :, :, :],
                                                      wt[:, :, :].unsqueeze(3).broadcast_to([P, JT, 2, E]), ALU.mult).then_inc(s_route_steps, 1)
                            dve.wait_ge(s_route_steps, ROUTE * b_d + 7)
                            V.tensor_tensor(rows[:, :, R_W:R_W + E], hw[:, :, 0, :], hw[:, :, 1, :], ALU.add).then_inc(s_route_steps, 1)
                            V.tensor_copy(rows[:, :, R_ID].bitcast(i32), tok[:, ds(b_d * JT, JT)]).then_inc(s_route_steps, 1)
                        if i == 16:
                            dve.wait_ge(s_rank_mm, b_d + 1)
                            if due(b_d):
                                dve.wait_ge(s_rank_read, b_d)
                            ps = J_b[bank_of("rank")]
                            V.tensor_tensor(pos8[:, :, :], ps[:, 0:JT * E].rearrange("p (j e) -> p j e", j=JT),
                                                      base[:, :].unsqueeze(1).broadcast_to([P, JT, E]), ALU.add).then_inc(s_route_steps, 1)
                            dve.wait_ge(s_route_steps, ROUTE * b_d + 10)
                            V.tensor_tensor(base[:, :], ps[:, JT * E:(JT + 1) * E], base[:, :], ALU.add).then_inc(
                                s_rank_read, 1)
                            V.tensor_tensor(hp[:, :, :, :], hot[:, :, :, :],
                                                      pos8[:, :, :].unsqueeze(2).broadcast_to([P, JT, 2, E]), ALU.mult).then_inc(s_route_steps, 1)
                            dve.wait_ge(s_route_steps, ROUTE * b_d + 11)
                            V.tensor_reduce(posf[:, :], hp[:, :, :, :].rearrange("p j k e -> p (j k) e"), X,
                                            ALU.add).then_inc(s_pos_f, 1)
                            dve.wait_ge(s_pos_f, b_d + 1)
                            if due(64 * b_d):
                                dve.wait_ge(s_scattered, 64 * b_d)
                            V.tensor_copy(pos[:, :], posf[:, :]).then_inc(s_pair_rows, 1)
                            
                    if e is not None and i in (7, 10, 13, 17):
                        w_low(e, (7, 10, 13, 17).index(i))
                    if b_s is not None and i < H:
                        dve.wait_ge(s_s_mm, H * b_s + i + 1)
                        if i == 0:
                            if due(b_s):
                                dve.wait_ge(s_maxT_mm, b_s)
                        V.tensor_reduce(mx[:, :].rearrange("p (s j h) -> p s j h", s=2, j=JT)[:, i % 2, :, i // 2],
                                        S_b[i % 2], X, ALU.max).then_inc(s_max_done, 1)
                    if b_c is not None and i >= LAG_PV and (i - LAG_PV) % 4 == 3:
                        g = (i - LAG_PV) // 4
                        dve.wait_ge(s_pv_mm, H * b_c + 4 * g + 4)
                        if due(4 * b_c + g):
                            dve.wait_ge(s_o_read, 4 * b_c + g)
                        V.reciprocal(rsum[:, :, :], O_b[g % 2][:, :, :, D]).then_inc(s_sums_inverted, 1)
                        dve.wait_ge(s_sums_inverted, 4 * b_c + g + 1)
                        if g == 0:
                            if due(b_c):
                                dve.wait_ge(s_oT_mm, b_c)
                        V.tensor_tensor(o_n[:, :, g * 4 * D:(g + 1) * 4 * D].rearrange("p j (h d) -> p j h d", h=4),
                                        O_b[g % 2][:, :, :, 0:D],
                                        rsum[:, :, :].unsqueeze(3).broadcast_to([P, JT, 4, D]), ALU.mult).then_inc(
                            s_o_read, 1)

            dve.wait_ge(s_iotas, 4)
            V.tensor_copy(base[:, :], region[:, :]).then_inc(s_base_set, 1)
            dve.wait_ge(s_base_set, 1)
            pipeline(dve, step)
            for e in range(PRE, E):
                for c in range(NCH):
                    w_low(e, c)

            dve.wait_ge(s_rank_read, B)
            dve.wait_ge(s_table_const, 1)
            V.tensor_copy(pad_at[:, :], base[0:1, :]).then_inc(s_table, 1)
            V.scalar_tensor_tensor(out=tni[:, 0, :], in0=base[0:1, :], scalar=float(P - 1), in1=region[0:1, :],
                                        op0=ALU.add, op1=ALU.subtract).then_inc(s_table_steps, 1)
            dve.wait_ge(s_table_steps, 1)
            V.tensor_scalar(tni[:, 1, :], tni[:, 0, :], 7, None, ALU.arith_shift_right).then_inc(s_table_steps, 1)
            dve.wait_ge(s_table_steps, 2)
            V.tensor_copy(tn[:, :], tni[:, 1, :]).then_inc(s_table_steps, 1)
            dve.wait_ge(s_table_steps, 3)
            V.tensor_tensor_scan(tcum[:, :], one8[:, :], tn[:, :], 0.0, ALU.mult, ALU.add).then_inc(s_table_steps, 1)
            dve.wait_ge(s_table_steps, 4)
            V.tensor_tensor(tle[:, :, :], tcum[:, :].unsqueeze(1).broadcast_to([1, NT, E]),
                                 tix[:, :].unsqueeze(2).broadcast_to([1, NT, E]), ALU.is_le).then_inc(s_table_steps, 1)
            dve.wait_ge(s_table_steps, 5)
            V.tensor_reduce(tex[:, :], tle[:, :, :], X, ALU.add).then_inc(s_table_steps, 1)
            dve.wait_ge(s_table_steps, 6)
            V.tensor_tensor(tlx[:, :, :], tle[:, :, :], tn[:, :].unsqueeze(1).broadcast_to([1, NT, E]), ALU.mult).then_inc(s_table_steps, 1)
            dve.wait_ge(s_table_steps, 7)
            V.tensor_reduce(tskip[:, :], tlx[:, :, :], X, ALU.add).then_inc(s_table_steps, 1)
            dve.wait_ge(s_table_steps, 8)
            V.tensor_tensor(trow[:, :], tix[:, :], tskip[:, :], ALU.subtract).then_inc(s_table_steps, 1)
            dve.wait_ge(s_table_steps, 9)
            V.tensor_scalar(trow[:, :], trow[:, :], float(P), None, ALU.mult).then_inc(s_table_steps, 1)
            dve.wait_ge(s_table_steps, 10)
            V.scalar_tensor_tensor(out=trow[:, :], in0=tex[:, :], scalar=float(REG), in1=trow[:, :],
                                        op0=ALU.mult, op1=ALU.add).then_inc(s_table_steps, 1)
            dve.wait_ge(s_table_steps, 11)
            V.tensor_scalar(tr_i[:, :], trow[:, :], float(E * REG), None, ALU.min).then_inc(s_table, 1)
            V.tensor_scalar(te_i[:, :], tex[:, :], float(E - 1), None, ALU.min).then_inc(s_table, 1)
            dve.wait_ge(s_table, 3)

            def split_hidden(t, p):
                for g in range(2):
                    m = slice(4 * g, 4 * g + 4)
                    dve.wait_ge(s_gelu_done, MC * t + 4 * g + 4)
                    if g == 0:
                        if due(t - 1):
                            dve.wait_ge(s_down_mm, t - 1)
                    V.tensor_scalar(hh[:, p, m, :], h32[:, p, m, :], HS, None, ALU.mult).then_inc(s_h_high, 1)
                    dve.wait_ge(s_h_high, 2 * t + g + 1)
                    V.scalar_tensor_tensor(out=hl[:, p, m, :], in0=h32[:, p, m, :], scalar=HS, in1=hh[:, p, m, :],
                                           op0=ALU.mult, op1=ALU.subtract).then_inc(s_h_split, 1)

            def weigh(t, p):
                e = dve.value_load(te_i[0:1, ds(t, 1)], min_val=0, max_val=E - 1)
                dve.wait_ge(s_down_mm, t + 1)
                if due(t):
                    dve.wait_ge(s_y_weighted, t)
                V.scalar_tensor_tensor(out=y[:, 2, :], in0=bank[4 + p][:, 0:C], scalar=1 / (HS * WS),
                                       in1=b2_bc[:, ds(e, 1), :].rearrange("p e c -> p (e c)"),
                                       op0=ALU.mult, op1=ALU.add).then_inc(s_y_read, 1)
                dve.wait_ge(s_y_read, t + 1)
                dve.wait_ge(s_meta_in, 16 * (t + 1))
                if due(16 * (t - 1)):
                    dve.wait_ge(s_summed, 16 * (t - 1))
                V.tensor_scalar(y[:, p, :], y[:, 2, :], meta[:, p, ds(e + 1, 1)], None, ALU.mult).then_inc(
                    s_y_weighted, 1)

            dve.wait_ge(s_b2_in, 16)
            split_hidden(0, 0)
            split_hidden(1, 1)
            weigh(0, 0)
            split_hidden(2, 0)
            weigh(1, 1)
            with dve.Fori(3, NT - 2, 2) as t:
                split_hidden(t, 1)
                weigh(t - 1, 0)
                split_hidden(t + 1, 0)
                weigh(t, 1)
            split_hidden(NT - 2, 1)
            weigh(NT - 3, 0)
            split_hidden(NT - 1, 0)
            weigh(NT - 2, 1)
            weigh(NT - 1, 0)

        @block.gpsimd
        def _(pool):
            G = nc.gpsimd
            G.iota(tok[:, :], pattern=[[P, TOK // P]], base=0, channel_multiplier=1).then_inc(s_iotas, 1)
            G.iota(expert_no[:, :], pattern=[[1, E]], base=0, channel_multiplier=0,
                   allow_small_or_imprecise_dtypes=True).then_inc(s_iotas, 1)
            G.iota(region[:, :], pattern=[[REG, E]], base=0, channel_multiplier=0,
                   allow_small_or_imprecise_dtypes=True).then_inc(s_iotas, 1)
            G.iota(tix[:, :], pattern=[[1, NT]], base=0, channel_multiplier=0,
                   allow_small_or_imprecise_dtypes=True).then_inc(s_iotas, 1)
            G.memset(id32[:, :], 0.0).then_inc(s_const_set, 1)
            G.memset(id16[:, :], 0.0).then_inc(s_const_set, 1)
            G.memset(tri[:, :], 1.0).then_inc(s_const_set, 1)
            G.memset(ones[:, :], 1.0).then_inc(s_consts, 1)
            G.memset(minus_half[:, :], -0.5).then_inc(s_const_set, 1)
            pool.wait_ge(s_const_set, 4)
            for m in (id32, id16):
                G.affine_select(out=m[:, :], in_=m[:, :], compare_op=ALU.not_equal, fill=1.0, base=0,
                                pattern=[[-1, P]], channel_multiplier=1).then_inc(s_consts, 1)
            G.affine_select(out=tri[:, :], in_=tri[:, :], compare_op=ALU.is_gt, fill=0.0, base=0,
                            pattern=[[1, P]], channel_multiplier=-1).then_inc(s_consts, 1)

            def inverse_root(dst, src, b, based, made):
                G.tensor_scalar(dst[:, :], src[:, :, 1], EPS, None, ALU.add).then_inc(based, 1)
                pool.wait_ge(based, apart(pool, b + 1))
                G.tensor_tensor(dst[:, :], dst[:, :], minus_half[:, :], ALU.pow).then_inc(made, 1)

            def step(t, static):
                b_a, b_s, b_c, b_d = stages(t, static)
                for i in range(SLOTS):
                    if b_a is not None and i == 0:
                        pool.wait_ge(s_ln1_steps, apart(pool, 2 * b_a + 2))
                        if due(2 * b_a):
                            pool.wait_ge(s_xn_done, apart(pool, 2 * b_a))
                        inverse_root(rstd, mv, b_a, s_rstd_base, s_rstd)
                    if b_d is not None:
                        if i == 4:
                            pool.wait_ge(s_x_res_in, apart(pool, 16 * (b_d + 1)))
                            pool.wait_ge(s_bo_in, 16)
                            G.tensor_tensor(x_res[:, :, :], x_res[:, :, :],
                                            bo_bc[:, :].unsqueeze(1).broadcast_to([P, JT, C]), ALU.add).then_inc(
                                s_x_res_bias, 1)
                        if i == 8:
                            pool.wait_ge(s_ln2_steps, apart(pool, LN2 * b_d + 2))
                            if due(b_d):
                                pool.wait_ge(s_row_parts, apart(pool, b_d))
                            inverse_root(rstd2, mv2, b_d, s_rstd2_base, s_rstd2)
                    if b_c is not None and LAG_ST <= i < H + LAG_ST:
                        h = i - LAG_ST
                        pool.wait_ge(s_exp_done, apart(pool, H * b_c + h + 1))
                        G.tensor_tensor(Pl[:, h % 4, :, :], Pe[:, h % 4, :, :],
                                        Pe[:, h % 4, :, :].bitcast(bf16)[:, :, 1::2], ALU.subtract).then_inc(
                            s_p_low, 1)
                    if b_d is not None and i == 18:
                        pool.wait_ge(s_pair_rows, apart(pool, b_d + 1))
                        pool.wait_ge(s_route_steps, apart(pool, ROUTE * (b_d + 1)))
                        for k in range(2 * JT):
                            G.indirect_dma_start(out=routed[:, :],
                                                 out_offset=bass.IndirectOffsetOnAxis(ap=pos[:, k:k + 1], axis=0),
                                                 in_=rows[:, k // 2, :], in_offset=None).then_inc(s_scattered, 16)

            pipeline(pool, step)

            def add_rows(t, p):
                pool.wait_ge(s_y_weighted, apart(pool, t + 1))
                if due(16 * t):
                    pool.wait_ge(s_summed, apart(pool, 16 * t))
                G.indirect_dma_start(out=acc[:, :],
                                     out_offset=bass.IndirectOffsetOnAxis(ap=meta[:, p, 0:1].bitcast(u32), axis=0),
                                     in_=y[:, p, :], in_offset=None, compute_op=ALU.add).then_inc(s_summed, 16)

            pool.wait_ge(s_x1_out, 16 * B)
            pool.wait_ge(s_acc_pad_out, 16)
            add_rows(0, 0)
            with pool.Fori(1, NT, 2) as t:
                add_rows(t, 1)
                add_rows(t + 1, 0)


_ARGS = ["x", "ctxT", "wqT", "wkT", "wvT", "woT", "bqk", "bv", "bo", "wrT", "w12", "b1", "b2"]


def kernel(x, ctx_1024, L0_xattn_Wq, L0_xattn_bq, L0_xattn_Wk, L0_xattn_bk, L0_xattn_Wv, L0_xattn_bv, L0_xattn_Wo,
           L0_xattn_bo, L0_ffn_Wr, L0_ffn_W1, L0_ffn_b1, L0_ffn_W2, L0_ffn_b2):
    import numpy as np
    import concourse.bacc as bacc
    from concourse.bass_utils import run_bass_kernel_spmd

    def flat(a):
        return np.ascontiguousarray(a)

    def by_partition(a, *lead):
        return flat(np.moveaxis(np.asarray(a).reshape(*lead, -1, P), -1, 0).reshape(P, -1))

    w1 = np.asarray(L0_ffn_W1).transpose(0, 2, 1).reshape(E, KC, P, M).transpose(0, 2, 1, 3).reshape(E, P, KC * M)
    w2 = np.asarray(L0_ffn_W2).transpose(0, 2, 1).reshape(E, MC, P, C).transpose(0, 2, 1, 3).reshape(E, P, MC * C)
    arrays = {
        "x": flat(np.asarray(x).reshape(TOK, C)),
        "ctxT": flat(np.asarray(ctx_1024).transpose(0, 2, 1)),
        "wqT": flat(np.asarray(L0_xattn_Wq).T),
        "wkT": flat(np.asarray(L0_xattn_Wk).T),
        "wvT": flat(np.asarray(L0_xattn_Wv).T),
        "woT": flat(np.asarray(L0_xattn_Wo).T),
        "bqk": flat(np.concatenate([by_partition(L0_xattn_bq), by_partition(L0_xattn_bk)], 1)),
        "bv": flat(L0_xattn_bv),
        "bo": flat(L0_xattn_bo),
        "wrT": flat(np.asarray(L0_ffn_Wr).T),
        "w12": flat(np.concatenate([w1, w2], 2)),
        "b1": by_partition(L0_ffn_b1, E),
        "b2": flat(L0_ffn_b2),
    }
    nc = bacc.Bacc("TRN2", target_bir_lowering=False, num_devices=1)
    args = [nc.dram_tensor(f"in_{n}", arrays[n].shape, mybir.dt.from_np(arrays[n].dtype), kind="ExternalInput").ap()
            for n in _ARGS]
    res = nc.dram_tensor("out_x", (B, N, C), mybir.dt.float32, kind="ExternalOutput").ap()
    cross_attention_moe(nc, *args, res)
    r = run_bass_kernel_spmd(nc, [{f"in_{n}": arrays[n] for n in _ARGS}], core_ids=[0])
    return r.results[0]["out_x"]
```

```python
import concourse.bass as bass
from concourse import mybir
from contextlib import ExitStack

B, N, C = 8, 256, 256
H = 16
D = C // H
E, M = 8, 1024
P = 128
KC = C // P
JT = N // P
MC = M // P
TOK = B * N
PAIRS = TOK * 2
NT = PAIRS // P + E - 1
REG = TOK + P
HR = 64
R3 = 3 * D
VW = D + 2
OW = D + 1
ROW = 272
R_ID, R_W = C, C + 1
EPS = 1e-5
XS, WS, HS = 1024.0, 512.0, 8.0
EW = 2 * 2 * KC * M
W2 = 2 * KC * M
CH = 1024
NCH = 2 * KC * M // CH
PRE = 6

LAG_ST, LAG_PV = 4, 6
SLOTS = H
WEIGHT_STEPS = (0, 1, 2, 3, 8, 9, 10)
W_SLOTS = (5, 8, 11, 14)
VR = 4
ON_DVE = (4, 7)
LN2, ROUTE = 3, 11
STEPS = B + 4


def cross_attention_moe(nc, x, ctxT, wqT, wkT, wvT, woT, bqkv, bo, wrT, w12, b1, b2, out):
    fp32, fp16, bf16 = mybir.dt.float32, mybir.dt.float16, mybir.dt.bfloat16
    i32, u32 = mybir.dt.int32, mybir.dt.uint32
    ALU, ACT, X = mybir.AluOpType, mybir.ActivationFunctionType, mybir.AxisListType.X
    ds = bass.ds

    q_st = nc.dram_tensor("q_stacked", (B, H, HR, N), fp16, kind="Internal").ap()
    k_st = nc.dram_tensor("k_stacked", (B, H, HR, N), fp16, kind="Internal").ap()
    routed = nc.dram_tensor("routed_rows", (E * REG + P, ROW), fp32, kind="Internal").ap()
    acc = nc.dram_tensor("accumulated", (TOK + P, C), fp32, kind="Internal").ap()

    with ExitStack() as ctx:
        def sb(name, shape, dt=fp32):
            return ctx.enter_context(nc.sbuf_tensor(name, shape, dt))

        Wx = sb("expert_weights", [P, E, EW], fp16)
        spare = Wx[:, PRE:E, :].rearrange("p e w -> p (e w)")
        NQ = 3 * H * N
        NV = VR * JT * H * VW
        Qs = spare[:, 0:NQ].rearrange("p (r h n) -> p r h n", r=3, h=H)
        Vh = spare[:, NQ:NQ + NV].rearrange("p (r j h d) -> p r j h d", r=VR, j=JT, h=H)

        AREA = 10240
        area = sb("area", [P, AREA])

        class Carve:
            def __init__(self):
                self.at = 0

            def __call__(self, words):
                self.at += words
                assert self.at <= AREA
                return area[:, self.at - words:self.at]

        a = Carve()
        Ks = a(3 * (H // 2) * N // 2).bitcast(fp16).rearrange("p (r h n) -> p r h n", r=3, h=H // 2)
        Pe = a(4 * JT * N).rearrange("p (r j n) -> p r j n", r=4, j=JT)
        Pl = a(4 * JT * N // 2).bitcast(fp16).rearrange("p (r j n) -> p r j n", r=4, j=JT)
        ctx_T = a(KC * N).rearrange("p (k n) -> p k n", k=KC)
        xnT = a(KC * N).rearrange("p (k n) -> p k n", k=KC)
        k16 = a(KC * N).bitcast(fp16).rearrange("p (s k n) -> p s k n", s=2, k=KC)
        q16 = a(KC * N).bitcast(fp16).rearrange("p (s k n) -> p s k n", s=2, k=KC)
        VAT = a.at
        Vl = a(VR * JT * C // 2).bitcast(fp16).rearrange("p (r j h d) -> p r j h d", r=VR, j=JT, h=H)
        o_n = a(JT * C).rearrange("p (j c) -> p j c", j=JT)
        oT = a(KC * N).rearrange("p (k n) -> p k n", k=KC)
        used = a.at
        f = Carve()
        b2_bc = f(E * C).rearrange("p (e c) -> p e c", e=E)
        xr = f(2 * C).rearrange("p (r c) -> p r c", r=2)
        meta = f(2 * 16).rearrange("p (r c) -> p r c", r=2)
        xT = f(2 * 2 * KC * P // 2).bitcast(fp16).rearrange("p (r s n) -> p r s n", r=2, s=2 * KC)
        h32 = f(2 * M).rearrange("p (r m n) -> p r m n", r=2, m=MC)
        hh = f(M).bitcast(fp16).rearrange("p (r m n) -> p r m n", r=2, m=MC)
        hl = f(M).bitcast(fp16).rearrange("p (r m n) -> p r m n", r=2, m=MC)
        y = f(3 * C).rearrange("p (r c) -> p r c", r=3)
        assert f.at <= VAT and used <= AREA

        x_in = sb("x_in", [P, JT, C])
        xn = sb("x_normed", [P, JT, C])
        x_res = sb("x_residual", [P, JT, C])
        x1 = sb("x_attended", [P, JT, C])
        xn2 = sb("x_attended_normed", [P, JT, C])
        rows = sb("rows", [P, JT, ROW])
        rows16 = rows[:, :, :].bitcast(fp16)
        pad = sb("pad_row", [P, ROW])
        xt2 = sb("x_attended_T", [P, JT, 2 * KC, P], fp16)
        wq, wk, wv, wo = (sb(n, [P, KC, C]) for n in ("wq", "wk", "wv", "wo"))
        stage = sb("weights_in", [P, 2, CH])
        bqkv_s = sb("bias_qkv", [P, 3 * KC])
        bo_row, ones_row = sb("bias_o", [1, C]), sb("ones_row", [1, P])
        b1_s = sb("bias_1", [P, E * MC])
        wr32 = sb("router_in", [P, KC, E])
        wr = sb("router", [P, 2, KC, E], fp16)
        id32, id16 = sb("ident32", [P, P]), sb("ident16", [P, P], fp16)
        tri, ones = sb("strict_tri", [P, P], bf16), sb("ones", [P, P], bf16)
        tok = sb("token", [P, TOK // P], i32)
        expert_no = sb("expert_no", [P, E])
        region = sb("region_start", [P, E])
        base = sb("next_row", [P, E])
        mx = sb("maxima", [P, 2 * JT * (H // 2)])
        mrow = sb("minus_max_rows", [2 * JT * (H // 2), P], fp16)
        minus_half = sb("minus_half", [P, JT])
        stats = sb("stats", [P, JT, 6])
        mv = sb("mean_var", [P, JT, 2])
        rstd = sb("rstd", [P, JT])
        shift = sb("minus_mean_rstd", [P, JT])
        stats2 = sb("stats2", [P, JT, 6])
        mv2 = sb("mean_var2", [P, JT, 2])
        rstd2 = sb("rstd2", [P, JT])
        shift2 = sb("minus_mean_rstd2", [P, JT])
        rsum = sb("one_by_sum", [P, JT, 4])
        lg = sb("logits", [P, JT, E])
        top = sb("top_logits", [P, JT, 8])
        topi = sb("top_index", [P, JT, 8], u32)
        topf = sb("top_index_f", [P, JT, 2])
        hot = sb("one_hot", [P, JT, 2, E])
        both = sb("both_hot", [P, JT, E], bf16)
        gap = sb("logit_gap", [P, JT])
        eg = sb("exp_gap", [P, JT])
        den = sb("denominator", [P, JT])
        wt = sb("pair_weight", [P, JT, 2])
        hw = sb("hot_weight", [P, JT, 2, E])
        pos8 = sb("rank_row", [P, JT, E])
        hp = sb("hot_row", [P, JT, 2, E])
        posf = sb("pair_row_f", [P, JT * 2])
        pos = sb("pair_row", [P, JT * 2], u32)
        tn, tni = sb("tiles_f", [1, E]), sb("tiles_i", [1, 2, E], i32)
        tcum = sb("tiles_cum", [1, E])
        one8 = sb("one8", [1, E])
        tix = sb("tile_no", [1, NT])
        tle, tlx = (area[0:1, VAT + i * NT * E:VAT + (i + 1) * NT * E].rearrange("p (t e) -> p t e", e=E)
                    for i in range(2))
        tex, trow = sb("tile_expert_f", [1, NT]), sb("tile_row_f", [1, NT])
        tskip = sb("tile_skip", [1, NT])
        te_i, tr_i = sb("tile_expert", [1, NT], i32), sb("tile_row", [1, NT], i32)
        pad_at = sb("pad_start", [1, E], i32)

        half_bank = [ctx.enter_context(nc.psum_tensor(f"banks{i}", [P, 1024], fp32)) for i in range(2)]
        bank = [half_bank[i // 2][:, (i % 2) * 512:(i % 2 + 1) * 512] for i in range(4)]
        bank += [ctx.enter_context(nc.psum_tensor(f"bank{i}", [P, 512], fp32)) for i in range(4, 8)]
        up_b = [half_bank[g][:, :].rearrange("p (m s n) -> p m s n", s=2, n=P) for g in range(2)]
        S_b = [bank[i][:, :].rearrange("p (j n) -> p j n", j=JT) for i in (0, 1)]
        T_b = [bank[i][:, :].rearrange("p (j n) -> p j n", j=JT) for i in (2, 3)]
        O_b = [bank[i][:, 0:JT * 4 * OW].rearrange("p (j h d) -> p j h d", j=JT, h=4) for i in (4, 5)]
        J_b = [bank[6], bank[7]]

        def semaphore(name):
            return ctx.enter_context(nc.semaphore(name))

        s_acc_pad_out, s_b1_in, s_b2_in, s_base_set, s_bo_in, s_both_hot, s_bqkv_in = (
            semaphore(n) for n in ("acc_pad_out", "b1_in", "b2_in", "base_set", "bo_in", "both_hot", "bqkv_in"))
        s_const_set, s_consts, s_ctx_in, s_down_mm, s_exp_done, s_exp_gap, s_gap, s_gelu_done = (
            semaphore(n) for n in ("const_set", "consts", "ctx_in", "down_mm", "exp_done", "exp_gap", "gap", "gelu_done"))
        s_h_high, s_h_split, s_iotas, s_k_back, s_k_mm, s_k_out, s_k_high, s_k_split = (
            semaphore(n) for n in ("h_high", "h_split", "iotas", "k_back", "k_mm", "k_out", "k_high", "k_split"))
        s_ln1_steps, s_ln2_steps, s_logit_mm, s_logit_read, s_maxT_mm, s_maxT_read, s_max_done, s_max_row_in = (
            semaphore(n) for n in ("ln1_steps", "ln2_steps", "logit_mm", "logit_read", "maxT_mm", "maxT_read", "max_done", "max_row_in"))
        s_meta_in, s_oT_mm, s_oT_read, s_o_read, s_out, s_p_low, s_pad_made, s_pad_out = (
            semaphore(n) for n in ("meta_in", "oT_mm", "oT_read", "o_read", "out", "p_low", "pad_made", "pad_out"))
        s_pad_zero, s_pair_rows, s_pair_weight, s_pos_f, s_pv_mm, s_q_back, s_q_mm, s_q_out = (
            semaphore(n) for n in ("pad_zero", "pair_rows", "pair_weight", "pos_f", "pv_mm", "q_back", "q_mm", "q_out"))
        s_q_high, s_q_split, s_q_zero_out, s_q_zero, s_k_ones, s_v_ones, s_rows_zero, s_p_low_v, s_rank_mm, s_rank_read, s_route_steps = (
            semaphore(n) for n in ("q_high", "q_split", "q_zero_out", "q_zero", "k_ones", "v_ones", "rows_zero", "p_low_v", "rank_mm", "rank_read", "route_steps"))
        s_router_split, s_rowT_mm, s_rowT_read, s_row_parts, s_rows_in, s_rstd, s_rstd2, s_xn2_done = (
            semaphore(n) for n in ("router_split", "rowT_mm", "rowT_read", "row_parts", "rows_in", "rstd", "rstd2", "xn2_done"))
        s_rooted, s_rooted2, s_ones_row, s_minus_half, s_row_high, s_s_mm, s_scattered, s_st_mm, s_summed, s_sums_inverted, s_table, s_table_const = (
            semaphore(n) for n in ("rooted", "rooted2", "ones_row", "minus_half", "row_high", "s_mm", "scattered", "st_mm", "summed", "sums_inverted", "table", "table_const"))
        s_table_steps, s_tile_T_mm, s_tile_T_read, s_up_mm, s_v_high, s_v_mm, s_v_split = (
            semaphore(n) for n in ("table_steps", "tile_T_mm", "tile_T_read", "up_mm", "v_high", "v_mm", "v_split"))
        s_w_high, s_w_low, s_wk_in, s_wo_in, s_wq_in, s_wr_in, s_wv_in, s_x1_mm = (
            semaphore(n) for n in ("w_high", "w_low", "wk_in", "wo_in", "wq_in", "wr_in", "wv_in", "x1_mm"))
        s_x1_out, s_x1_read, s_xT_mm, s_xT_read, s_x_in, s_x_res_in, s_xn_done = (
            semaphore(n) for n in ("x1_out", "x1_read", "xT_mm", "xT_read", "x_in", "x_res_in", "xn_done"))
        s_y_high, s_y_read, s_y_weighted, s_up_read, s_h_low = (
            semaphore(n) for n in ("y_high", "y_read", "y_weighted", "up_read", "h_low"))
        s_w_in = [semaphore(f"w_in{i}") for i in range(2)]

        def due(value):
            return not isinstance(value, int) or value > 0

        def apart(eng, value):
            if isinstance(value, int):
                return value
            held = eng.to_reg(value)
            eng.wait_ge(s_iotas, 4)
            return held

        def halves(e, c):
            if c < NCH // 2:
                both_at = Wx[:, ds(e, 1), 0:W2].rearrange("p e (s w) -> p (e s) w", s=2)
                return [both_at[:, s, c * CH:(c + 1) * CH] for s in range(2)]
            at = W2 + (c - NCH // 2) * 2 * CH
            both_at = Wx[:, ds(e, 1), at:at + 2 * CH].rearrange("p e (m s w) -> p (e m) s w", s=2, w=C)
            return [both_at[:, :, s, :] for s in range(2)]

        def staged(c, like):
            return stage[:, c % 2, :] if len(like.shape) == 2 else stage[:, c % 2, :].rearrange("p (m w) -> p m w", w=C)

        uses = [("maxT", 1, 2, s_maxT_read), ("logit", 0, 4, s_logit_read), ("k", 1, 0, s_k_split),
                ("v", 0, 0, s_v_split), ("rank", 1, 4, s_rank_read), ("xT", 0, 0, s_xT_read), ("oT", 1, 3, s_oT_read),
                ("q", 0, 0, s_q_split), ("x1", 1, 3, s_x1_read), ("rowT", 0, 3, s_rowT_read)]

        def bank_of(name):
            return next(u[1] for u in uses if u[0] == name)

        def bank_user_before(name, t, static):
            at = next(i for i, u in enumerate(uses) if u[0] == name)
            step, i = 0, at
            while True:
                i -= 1
                if i < 0:
                    i, step = len(uses) - 1, step + 1
                _, bank_no, stage, read = uses[i]
                if static and t - step < 0:
                    return None
                if bank_no == uses[at][1] and (not static or 0 <= t - step - stage < B):
                    return read, t - step - stage + 1

        def stages(t, static):
            return [t - s if not static or 0 <= t - s < B else None for s in range(5)]

        def head_at(i, lag, b_c, b_d):
            return (b_c, i - lag) if i >= lag else (b_d, H + i - lag)

        def p_low_count(b, h):
            mine = [g for g in range(H) if (g in ON_DVE) == (h in ON_DVE)]
            return (s_p_low_v if h in ON_DVE else s_p_low), len(mine) * b + mine.index(h) + 1

        def pipeline(eng, step, end=B):
            for t in range(5):
                step(t, True)
            with eng.Fori(5, end) as t:
                step(t, False)
            for t in range(end, STEPS):
                step(t, True)

        def expert_of(t, static):
            return WEIGHT_STEPS.index(t) if static and t in WEIGHT_STEPS else None

        def p_low(engine, h):
            return engine.tensor_tensor(Pl[:, h % 4, :, :], Pe[:, h % 4, :, :],
                                        Pe[:, h % 4, :, :].bitcast(bf16)[:, :, 1::2], ALU.subtract)

        block = ctx.enter_context(nc.Block())

        @block.sync
        def _(sp):
            def load_x(b):
                sp.dma_start(x_in[:, :, :],
                             x[ds(b * N, N), :].rearrange("(j p) c -> p j c", p=P)).then_inc(s_x_in, 16)

            def load_ctx(b):
                sp.dma_start(ctx_T,
                             ctxT[ds(b, 1), :, :].rearrange("b (k p) n -> p (b k) n", p=P)).then_inc(s_ctx_in, 16)

            load_x(0)
            load_ctx(0)
            sp.dma_start(wk[:, :, :], wkT.rearrange("(k p) c -> p k c", p=P)).then_inc(s_wk_in, 16)
            sp.dma_start(bqkv_s[:, :], bqkv).then_inc(s_bqkv_in, 16)
            sp.dma_start(wv[:, :, :], wvT.rearrange("(k p) c -> p k c", p=P)).then_inc(s_wv_in, 16)
            sp.dma_start(wq[:, :, :], wqT.rearrange("(k p) c -> p k c", p=P)).then_inc(s_wq_in, 16)
            sp.dma_start(wo[:, :, :], woT.rearrange("(k p) c -> p k c", p=P)).then_inc(s_wo_in, 16)
            sp.dma_start(bo_row[:, :], bo.rearrange("(o c) -> o c", o=1)).then_inc(s_bo_in, 16)
            sp.dma_start(wr32[:, :, :], wrT.rearrange("(k p) e -> p k e", p=P)).then_inc(s_wr_in, 16)
            sp.dma_start(b1_s[:, :], b1).then_inc(s_b1_in, 16)
            sp.wait_ge(s_pad_made, 2)
            sp.dma_start(q_st[:, :, R3, :].rearrange("b h n -> (b h) n"),
                         pad[:, 0:N // 2].bitcast(fp16)).then_inc(s_q_zero_out, 16)
            sp.dma_start(routed[E * REG:E * REG + P, :], pad[:, :]).then_inc(s_pad_out, 16)
            sp.dma_start(acc[TOK:TOK + P, :], pad[:, 0:C]).then_inc(s_acc_pad_out, 16)

            def load_weights(e, c):
                n = NCH * e + c
                if due(n - 1):
                    sp.wait_ge(s_w_high, apart(sp, n - 1))
                if due(n - 1):
                    sp.wait_ge(s_w_low, apart(sp, n - 1))
                sp.dma_start(stage[:, c % 2, :],
                             w12[ds(e, 1), :, c * CH:(c + 1) * CH].rearrange("e p w -> (e p) w")).then_inc(s_w_in[c % 2], 16)

            def step(t, static):
                b_a, b_s, b_c, b_d, b_e = stages(t, static)
                e = expert_of(t, static)
                if e is not None:
                    load_weights(e, 0)
                    load_weights(e, 1)
                if b_d is not None:
                    if due(b_d):
                        sp.wait_ge(s_x1_read, apart(sp, b_d))
                    sp.dma_start(x_res[:, :, :],
                                 x[ds(b_d * N, N), :].rearrange("(j p) c -> p j c", p=P)).then_inc(s_x_res_in, 16)
                if b_c is not None:
                    sp.wait_ge(s_maxT_read, apart(sp, b_c + 1))
                    if due(64 * b_c):
                        sp.wait_ge(s_max_row_in, apart(sp, 64 * b_c))
                    for s in range(2):
                        for j in range(JT):
                            at = (s * JT + j) * (H // 2)
                            sp.dma_start(Qs[s * HR + R3:s * HR + R3 + 1, ds(b_c % 3, 1), s::2,
                                            j * P:(j + 1) * P].rearrange("p r h n -> p (r h) n"),
                                         mrow[at:at + H // 2, :]).then_inc(s_max_row_in, 16)
                if b_a is not None:
                    sp.wait_ge(s_k_split, apart(sp, b_a + 1))
                    for r, part in enumerate((0, 1, 0)):
                        for c in range(KC):
                            sp.dma_start(k_st[ds(b_a, 1), c * 8:c * 8 + 8, r * D:(r + 1) * D, :].rearrange("b h d n -> (b h) d n"),
                                         k16[:, part, c, :]).then_inc(s_k_out, 16)
                    sp.wait_ge(s_k_out, apart(sp, 96 * (b_a + 1)))
                    if due(16 * b_a):
                        sp.wait_ge(s_k_back, apart(sp, 16 * b_a))
                    if due(H * (b_a - 2)):
                        sp.wait_ge(s_st_mm, apart(sp, H * (b_a - 2)))
                    sp.wait_ge(s_k_ones, 1)
                    src = k_st[ds(b_a, 1), :, 0:R3, :].rearrange("b (h s) r n -> s r (b h) n", s=2)
                    for s in range(2):
                        sp.dma_start(Ks[s * HR:s * HR + R3, ds(b_a % 3, 1), :, :].rearrange("p r h n -> p (r h) n"),
                                     src[s]).then_inc(s_k_back, 16)
                if e is not None:
                    load_weights(e, 2)
                if b_a is not None:
                    sp.wait_ge(s_q_split, apart(sp, b_a + 1))
                    for r, part in enumerate((0, 0, 1)):
                        for c in range(KC):
                            sp.dma_start(q_st[ds(b_a, 1), c * 8:c * 8 + 8, r * D:(r + 1) * D, :].rearrange("b h d n -> (b h) d n"),
                                         q16[:, part, c, :]).then_inc(s_q_out, 16)
                if e is not None:
                    load_weights(e, 3)
                if b_a is not None and (not static or b_a < B - 1):
                    sp.wait_ge(s_xn_done, apart(sp, 2 * (b_a + 1)))
                    load_x(b_a + 1)
                    sp.wait_ge(s_v_mm, apart(sp, b_a + 1))
                    load_ctx(b_a + 1)
                if b_a is not None:
                    sp.wait_ge(s_q_out, apart(sp, 96 * (b_a + 1)))
                    sp.wait_ge(s_q_zero_out, 16)
                    sp.wait_ge(s_q_zero, 1)
                    if due(32 * b_a):
                        sp.wait_ge(s_q_back, apart(sp, 32 * b_a))
                    src = q_st[ds(b_a, 1), :, 0:R3 + 1, :].rearrange("b (h s) r n -> s r (b h) n", s=2)
                    for s in range(2):
                        sp.dma_start(Qs[s * HR:s * HR + R3 + 1, ds(b_a % 3, 1), s::2, :].rearrange("p r h n -> p (r h) n"),
                                     src[s]).then_inc(s_q_back, 16)
                if b_d is not None:
                    sp.wait_ge(s_x1_read, apart(sp, b_d + 1))
                    sp.dma_start(acc[ds(b_d * N, N), :].rearrange("(j p) c -> p j c", p=P),
                                 x1[:, :, :]).then_inc(s_x1_out, 16)
            pipeline(sp, step, B - 1)
            sp.wait_ge(s_pv_mm, H * B)
            sp.dma_start(b2_bc,
                         b2.rearrange("(o e) c -> o (e c)", o=1)[0].partition_broadcast(P).rearrange("p (e c) -> p e c", e=E)).then_inc(s_b2_in, 16)
            for c in range(2):
                load_weights(E - 1, c)
            sp.wait_ge(s_table, 3)
            sp.wait_ge(s_pad_out, 16)
            for e in range(0, E, 2):
                row = sp.value_load(pad_at[0:1, e:e + 1], min_val=0, max_val=E * REG - P)
                sp.dma_start(routed[ds(row, P), :], pad[:, :]).then_inc(s_pad_out, 16)
            for c in range(2, NCH):
                load_weights(E - 1, c)
            sp.wait_ge(s_pad_out, 16 * (E + 1))
            sp.wait_ge(s_scattered, 64 * B)

            def rows_in(t, p):
                at = sp.value_load(tr_i[0:1, ds(t, 1)], min_val=0, max_val=E * REG)
                if due(t - 1):
                    sp.wait_ge(s_tile_T_mm, apart(sp, t - 1))
                if due(16 * t):
                    sp.wait_ge(s_rows_in, apart(sp, 16 * t))
                sp.dma_start(xr[:, p, :], routed[ds(at, P), 0:C]).then_inc(s_rows_in, 16)

            def meta_in(t, p):
                at = sp.value_load(tr_i[0:1, ds(t, 1)], min_val=0, max_val=E * REG)
                if due(16 * (t - 1)):
                    sp.wait_ge(s_summed, apart(sp, 16 * (t - 1)))
                if due(16 * t):
                    sp.wait_ge(s_meta_in, apart(sp, 16 * t))
                sp.dma_start(meta[:, p, 0:E + 1], routed[ds(at, P), R_ID:R_ID + E + 1]).then_inc(s_meta_in, 16)

            rows_in(0, 0)
            rows_in(1, 1)
            meta_in(0, 0)
            rows_in(2, 0)
            meta_in(1, 1)
            with sp.Fori(3, NT - 1, 2) as t:
                rows_in(t, 1)
                meta_in(t - 1, 0)
                rows_in(t + 1, 0)
                meta_in(t, 1)
            meta_in(NT - 1, 0)
            sp.wait_ge(s_summed, 16 * NT)
            sp.dma_start(out.rearrange("b n c -> (b n) c"), acc[0:TOK, :]).then_inc(s_out, 16)
            sp.wait_ge(s_out, 16)

        @block.tensor
        def _(pe):
            mm = nc.tensor.matmul

            def attend_scores(b, h):
                if h == 0:
                    pe.wait_ge(s_k_back, 32 * (b + 1))
                    pe.wait_ge(s_q_back, 32 * (b + 1))
                if due(H * b + h - 1):
                    pe.wait_ge(s_max_done, H * b + h - 1)
                for j in range(JT):
                    last = mm(S_b[h % 2][:, j, :], Qs[:, ds(b % 3, 1), h, j * P:(j + 1) * P],
                              Ks[:, ds(b % 3, 1), h // 2, :], start=True, stop=True)
                last.then_inc(s_s_mm, 1)

            def attend_scores_T(b, h):
                if h == 0:
                    pe.wait_ge(s_max_row_in, 64 * (b + 1))
                if due(H * b + h - 1):
                    pe.wait_ge(s_exp_done, H * b + h - 1)
                for j in range(JT):
                    last = mm(T_b[h % 2][:, j, :], Ks[:, ds(b % 3, 1), h // 2, j * P:(j + 1) * P],
                              Qs[:, ds(b % 3, 1), h, :], start=True, stop=True)
                last.then_inc(s_st_mm, 1)

            def attend_values(b, h):
                if h % 4 == 0:
                    if due(4 * b + h // 4 - 1):
                        pe.wait_ge(s_o_read, 4 * b + h // 4 - 1)
                if h == 0:
                    pe.wait_ge(s_v_split, b + 1)
                    pe.wait_ge(s_v_high, b + 1)
                    pe.wait_ge(s_v_ones, 1)
                pe.wait_ge(*p_low_count(b, h))
                ph = Pe[:, h % 4, :, :].bitcast(bf16)
                for j in range(JT):
                    o = O_b[(h // 4) % 2][:, j, h % 4, :]
                    for k in range(JT):
                        hi = ph[:, k, 2 * j * P + 1:2 * (j + 1) * P:2]
                        v_hi = Vh[:, ds(b % VR, 1), k, h, 0:OW]
                        mm(o, hi, v_hi, start=k == 0, stop=False)
                        mm(o[:, 0:D], hi, Vl[:, ds(b % VR, 1), k, h, :], start=False, stop=False)
                        last = mm(o, Pl[:, h % 4, k, j * P:(j + 1) * P], v_hi, start=False, stop=k == JT - 1)
                last.then_inc(s_pv_mm, 1)

            def project_T(name, w, src, made, t, static):
                if before := bank_user_before(name, t, static):
                    pe.wait_ge(*before)
                ps = J_b[bank_of(name)][:, :].rearrange("p (c n) -> p c n", c=KC)
                for c in range(KC):
                    for k in range(KC):
                        last = mm(ps[:, c, :], w[:, k, c * P:(c + 1) * P], src[:, k, :], start=k == 0, stop=k == KC - 1)
                last.then_inc(made, 1)

            def project(name, w, src, made, t, static, bias=None):
                if before := bank_user_before(name, t, static):
                    pe.wait_ge(*before)
                ps = J_b[bank_of(name)][:, :].rearrange("p (j c) -> p j c", j=JT)
                for j in range(JT):
                    for k in range(KC):
                        last = mm(ps[:, j, :], src[:, k, j * P:(j + 1) * P], w[:, k, :], start=k == 0,
                                  stop=k == KC - 1 and bias is None)
                    if bias is not None:
                        last = mm(ps[:, j, :], ones_row[:, :], bias[:, :], start=False, stop=True)
                last.then_inc(made, 1)

            def transposed(name, src, made, t, static):
                if before := bank_user_before(name, t, static):
                    pe.wait_ge(*before)
                ps = J_b[bank_of(name)][:, :].rearrange("p (k n) -> p k n", k=KC)
                for k in range(KC):
                    for j in range(JT):
                        last = nc.tensor.transpose(ps[:, k, j * P:(j + 1) * P], src[:, j, k * P:(k + 1) * P], id32[:, :])
                last.then_inc(made, 1)

            def step(t, static):
                b_a, b_s, b_c, b_d, b_e = stages(t, static)
                for i in range(SLOTS):
                    if b_s is not None:
                        attend_scores(b_s, i)
                    b, h = head_at(i, LAG_ST, b_c, b_d)
                    if b is not None:
                        attend_scores_T(b, h)
                    if b_e is not None and i == 1:
                        if before := bank_user_before("logit", t, static):
                            pe.wait_ge(*before)
                        pe.wait_ge(s_rowT_read, b_e + 1)
                        pe.wait_ge(s_router_split, 2)
                        for j in range(JT):
                            ps = J_b[bank_of("logit")][:, j * E:(j + 1) * E]
                            for k in range(KC):
                                mm(ps, xt2[:, j, k, :], wr[:, 0, k, :], start=k == 0, stop=False)
                                mm(ps, xt2[:, j, k, :], wr[:, 1, k, :], start=False, stop=False)
                                last = mm(ps, xt2[:, j, KC + k, :], wr[:, 0, k, :], start=False, stop=k == KC - 1)
                        last.then_inc(s_logit_mm, 1)
                    if b_a is not None:
                        if i == 2:
                            pe.wait_ge(s_ctx_in, 16 * (b_a + 1))
                            pe.wait_ge(s_wk_in, 16)
                            project_T("k", wk, ctx_T, s_k_mm, t, static)
                    if b_c is not None and i == 0:
                        if before := bank_user_before("maxT", t, static):
                            pe.wait_ge(*before)
                        pe.wait_ge(s_max_done, H * (b_c + 1))
                        nc.tensor.transpose(J_b[bank_of("maxT")][0:32, 0:P], mx[:, :], id32[:, :]).then_inc(
                            s_maxT_mm, 1)
                    if b_a is not None and i == 4:
                        pe.wait_ge(s_wv_in, 16)
                        project("v", wv, ctx_T, s_v_mm, t, static)
                    if b_e is not None and i == 5:
                        if before := bank_user_before("rank", t, static):
                            pe.wait_ge(*before)
                        pe.wait_ge(s_both_hot, b_e + 1)
                        ps = J_b[bank_of("rank")]
                        mm(ps[:, 0:E], tri[:, :], both[:, 0, :], start=True, stop=True)
                        mm(ps[:, E:2 * E], tri[:, :], both[:, 1, :], start=True, stop=False)
                        mm(ps[:, E:2 * E], ones[:, :], both[:, 0, :], start=False, stop=True)
                        mm(ps[:, 2 * E:3 * E], ones[:, :], both[:, 0, :], start=True, stop=False)
                        mm(ps[:, 2 * E:3 * E], ones[:, :], both[:, 1, :], start=False, stop=True).then_inc(
                            s_rank_mm, 1)
                    if b_d is not None and i == 7:
                        pe.wait_ge(s_o_read, 4 * (b_d + 1))
                        transposed("oT", o_n, s_oT_mm, t, static)
                    if b_a is not None:
                        if i == 6:
                            pe.wait_ge(s_xn_done, 2 * (b_a + 1))
                            pe.wait_ge(s_consts, 4)
                            transposed("xT", xn, s_xT_mm, t, static)
                        if i == 8:
                            pe.wait_ge(s_xT_read, b_a + 1)
                            pe.wait_ge(s_wq_in, 16)
                            project_T("q", wq, xnT, s_q_mm, t, static)
                    if b_d is not None:
                        if i == 9:
                            pe.wait_ge(s_oT_read, b_d + 1)
                            pe.wait_ge(s_wo_in, 16)
                            pe.wait_ge(s_bo_in, 16)
                            pe.wait_ge(s_ones_row, 1)
                            project("x1", wo, oT, s_x1_mm, t, static, bo_row)
                        if i == 15:
                            if before := bank_user_before("rowT", t, static):
                                pe.wait_ge(*before)
                            pe.wait_ge(s_row_parts, b_d + 1)
                            ps = J_b[bank_of("rowT")][:, :].bitcast(fp16).rearrange("p (j s n) -> p j s n", j=JT, s=4)
                            for j in range(JT):
                                for s in range(2 * KC):
                                    last = nc.tensor.transpose(ps[:, j, s, :], rows16[:, j, s * P:(s + 1) * P], id16[:, :])
                            last.then_inc(s_rowT_mm, 1)
                    b, h = head_at(i, LAG_PV, b_c, b_d)
                    if b is not None:
                        attend_values(b, h)

            pipeline(pe, step)

            def tile_T(t, p):
                pe.wait_ge(s_rows_in, 16 * (t + 1))
                if due(t):
                    pe.wait_ge(s_tile_T_read, t)
                ps = bank[6][:, 0:2 * P].bitcast(fp16).rearrange("p (s n) -> p s n", s=2 * KC)
                src = xr[:, p, :].bitcast(fp16)
                for s in range(2 * KC):
                    last = nc.tensor.transpose(ps[:, s % KC * 2 + s // KC, :], src[:, s * P:(s + 1) * P], id16[:, :])
                last.then_inc(s_tile_T_mm, 1)

            def expert_at(t):
                return pe.value_load(te_i[0:1, ds(t, 1)], min_val=0, max_val=E - 1)

            def up(t, p, e):
                pe.wait_ge(s_tile_T_read, t + 1)
                for m in range(MC):
                    if m % 4 == 0:
                        if due(2 * (t - 1) + m // 4 + 1):
                            pe.wait_ge(s_up_read, 2 * (t - 1) + m // 4 + 1)
                    ps = up_b[m // 4][:, m % 4, :, :].rearrange("p s n -> p (s n)")
                    for k in range(KC):
                        at = k * M + m * P
                        hi, lo = Wx[:, ds(e, 1), at:at + P], Wx[:, ds(e, 1), KC * M + at:KC * M + at + P]
                        if k > 0:
                            mm(ps[:, 0:P], lo, xT[:, p, 2 * k, :], start=False, stop=False)
                        last = mm(ps, hi, xT[:, p, 2 * k:2 * k + 2, :], start=k == 0, stop=k == KC - 1)
                        if k == 0:
                            mm(ps[:, 0:P], lo, xT[:, p, 2 * k, :], start=False, stop=False)
                    if m % 4 == 3:
                        last.then_inc(s_up_mm, 1)

            def down(t, p, e, load=None):
                if due(t - 1):
                    pe.wait_ge(s_y_read, t - 1)
                ps = bank[4 + p]
                loaded = None
                for m in range(MC):
                    if m == MC // 2 and load is not None:
                        loaded = expert_at(load)
                    if m % 4 == 0:
                        pe.wait_ge(s_h_split, 2 * t + m // 4 + 1)
                    at = W2 + m * 2 * C
                    if m > 0:
                        mm(ps[:, 0:C], hl[:, p, m, :], Wx[:, ds(e, 1), at:at + C], start=False, stop=False)
                    last = mm(ps[:, :], hh[:, p, m, :], Wx[:, ds(e, 1), at:at + 2 * C], start=m == 0, stop=m == MC - 1)
                    if m == 0:
                        mm(ps[:, 0:C], hl[:, p, m, :], Wx[:, ds(e, 1), at:at + C], start=False, stop=False)
                last.then_inc(s_down_mm, 1)
                return loaded

            pe.wait_ge(s_table, 3)
            pe.wait_ge(s_w_high, NCH * E)
            pe.wait_ge(s_w_low, NCH * E)
            e0 = expert_at(0)
            tile_T(0, 0)
            up(0, 0, e0)
            e1 = expert_at(1)
            tile_T(1, 1)
            up(1, 1, e1)
            tile_T(2, 0)
            e2 = down(0, 0, e0, load=2)
            up(2, 0, e2)
            tile_T(3, 1)
            down(1, 1, e1)

            def two_tiles(t, before, this):
                up(t, 1, this)
                tile_T(t + 1, 0)
                after = down(t - 1, 0, before, load=t + 1)
                up(t + 1, 0, after)
                tile_T(t + 2, 1)
                return after, down(t, 1, this, load=t + 2)

            with pe.Fori(3, NT - 4, 4) as t:
                experts = expert_at(t - 1), expert_at(t)
                for ahead in range(0, 4, 2):
                    experts = two_tiles(t + ahead, *experts)
            before, this = two_tiles(NT - 4, expert_at(NT - 5), expert_at(NT - 4))
            up(NT - 2, 1, this)
            tile_T(NT - 1, 0)
            after = down(NT - 3, 0, before, load=NT - 1)
            up(NT - 1, 0, after)
            down(NT - 2, 1, this)
            down(NT - 1, 0, after)

        @block.scalar
        def _(act):
            A = nc.scalar.activation

            def heads_T(name, dst, first):
                ps = J_b[bank_of(name)][:, :].rearrange("p (c n) -> p c n", c=KC)
                for c in range(KC):
                    last = A(dst[:, 0, c, :], ps[:, c, :], ACT.Identity, bias=bqkv_s[:, first + c:first + c + 1])
                return last

            def w_high(e, c):
                n = NCH * e + c
                act.wait_ge(s_w_in[c % 2], 32 * e + 16 * (c // 2 + 1))
                hi = halves(e, c)[0]
                A(hi, staged(c, hi), ACT.Copy, scale=WS).then_inc(s_w_high, 1)

            def step(t, static):
                b_a, b_s, b_c, b_d, b_e = stages(t, static)
                e = expert_of(t, static)
                for i in range(SLOTS):
                    b, h = head_at(i, LAG_ST, b_c, b_d)
                    if b is not None:
                        act.wait_ge(s_st_mm, H * b + h + 1)
                        if due(H * b + h - 3):
                            act.wait_ge(s_pv_mm, H * b + h - 3)
                        A(Pe[:, h % 4, :, :], T_b[h % 2], ACT.Exp, scale=float(D) ** -0.5).then_inc(s_exp_done, 1)
                    if b_c is not None and i == 0:
                        act.wait_ge(s_maxT_mm, b_c + 1)
                        if due(64 * b_c):
                            act.wait_ge(s_max_row_in, 64 * b_c)
                        A(mrow[:, :], J_b[bank_of("maxT")][0:32, 0:P], ACT.Copy, scale=-1.0).then_inc(s_maxT_read, 1)
                    if b_a is not None:
                        if i == 2:
                            act.wait_ge(s_k_mm, b_a + 1)
                            act.wait_ge(s_bqkv_in, 16)
                            if due(b_a):
                                act.wait_ge(s_k_out, 96 * b_a)
                            heads_T("k", k16, KC).then_inc(s_k_high, 1)
                        if i == 4:
                            act.wait_ge(s_v_mm, b_a + 1)
                            if due(H * (b_a - 3)):
                                act.wait_ge(s_pv_mm, H * (b_a - 3))
                            A(Vh[:, ds(b_a % VR, 1), :, :, 0:D].rearrange("p r j h d -> p (r j) h d"),
                              J_b[bank_of("v")][:, :].rearrange("p (j h d) -> p j h d", j=JT, h=H), ACT.Copy).then_inc(
                                s_v_high, 1)
                        if i == 3:
                            act.wait_ge(s_rstd, b_a + 1)
                            if due(b_a):
                                act.wait_ge(s_xT_mm, b_a)
                            for j in range(JT):
                                A(xn[:, j, :], x_in[:, j, :], ACT.Identity, bias=shift[:, j:j + 1],
                                  scale=rstd[:, j:j + 1]).then_inc(s_xn_done, 1)
                        if i == 6:
                            act.wait_ge(s_xT_mm, b_a + 1)
                            if due(b_a):
                                act.wait_ge(s_q_mm, b_a)
                            A(xnT, J_b[bank_of("xT")][:, :].rearrange("p (k n) -> p k n", k=KC), ACT.Copy).then_inc(
                                s_xT_read, 1)
                        if i == 8:
                            act.wait_ge(s_q_mm, b_a + 1)
                            if due(b_a):
                                act.wait_ge(s_q_out, 96 * b_a)
                            heads_T("q", q16, 0).then_inc(s_q_high, 1)
                    if b_e is not None and i == 3:
                        act.wait_ge(s_gap, b_e + 1)
                        if due(b_e):
                            act.wait_ge(s_pair_weight, b_e)
                        A(eg[:, :], gap[:, :], ACT.Exp).then_inc(s_exp_gap, 1)
                    if b_d is not None:
                        if i == 7:
                            act.wait_ge(s_oT_mm, b_d + 1)
                            act.wait_ge(s_bqkv_in, 16)
                            if due(b_d):
                                act.wait_ge(s_x1_mm, b_d)
                            ps = J_b[bank_of("oT")][:, :].rearrange("p (k n) -> p k n", k=KC)
                            for k in range(KC):
                                last = A(oT[:, k, :], ps[:, k, :], ACT.Identity, bias=bqkv_s[:, 2 * KC + k:2 * KC + k + 1])
                            last.then_inc(s_oT_read, 1)
                        if i == 12:
                            act.wait_ge(s_rstd2, b_d + 1)
                            if due(b_d):
                                act.wait_ge(s_row_parts, b_d)
                            for j in range(JT):
                                A(xn2[:, j, :], x1[:, j, :], ACT.Identity, bias=shift2[:, j:j + 1],
                                  scale=rstd2[:, j:j + 1]).then_inc(s_xn2_done, 1)
                        if i == 15:
                            act.wait_ge(s_rowT_mm, b_d + 1)
                            if due(b_d):
                                act.wait_ge(s_logit_mm, b_d)
                            ps = J_b[bank_of("rowT")][:, :].bitcast(fp16).rearrange("p (j s n) -> p j s n", j=JT, s=4)
                            A(xt2[:, :, :, :], ps, ACT.Copy).then_inc(s_rowT_read, 1)
                    if e is not None and i in W_SLOTS:
                        if static and t == STEPS - 2 and i == W_SLOTS[0]:
                            act.wait_ge(s_pv_mm, H * B)
                        w_high(e, W_SLOTS.index(i))

            pipeline(act, step)
            for c in range(2):
                w_high(E - 1, c)
            act.wait_ge(s_table, 3)
            act.wait_ge(s_pad_made, 2)
            for e in range(1, E, 2):
                row = act.value_load(pad_at[0:1, e:e + 1], min_val=0, max_val=E * REG - P)
                act.dma_start(routed[ds(row, P), :], pad[:, :]).then_inc(s_pad_out, 16)
            for c in range(2, NCH):
                w_high(E - 1, c)

            def copy_T(t, p):
                act.wait_ge(s_tile_T_mm, t + 1)
                if due(2 * (t - 1)):
                    act.wait_ge(s_up_mm, 2 * (t - 1))
                ps = bank[6][:, 0:2 * P].bitcast(fp16).rearrange("p (s n) -> p s n", s=2 * KC)
                A(xT[:, p, :, :], ps, ACT.Copy).then_inc(s_tile_T_read, 1)

            def hidden_low(t, p):
                for g in range(2):
                    act.wait_ge(s_up_mm, 2 * t + g + 1)
                    if due(2 * (t - 2) + g + 1):
                        act.wait_ge(s_h_split, 2 * (t - 2) + g + 1)
                    A(h32[:, p, 4 * g:4 * g + 4, :], up_b[g][:, :, 1, :], ACT.Copy).then_inc(s_h_low, 1)

            def gelu(t, p):
                e = act.value_load(te_i[0:1, ds(t, 1)], min_val=0, max_val=E - 1)
                for m in range(MC):
                    if m % 4 == 0:
                        act.wait_ge(s_up_read, 2 * t + m // 4 + 1)
                    A(h32[:, p, m, :], h32[:, p, m, :], ACT.Gelu, bias=b1_s[:, ds(e * MC + m, 1)],
                      scale=1 / (XS * WS)).then_inc(s_gelu_done, 1)

            act.wait_ge(s_table, 3)
            act.wait_ge(s_b1_in, 16)
            copy_T(0, 0)
            hidden_low(0, 0)
            copy_T(1, 1)
            gelu(0, 0)
            hidden_low(1, 1)
            copy_T(2, 0)
            gelu(1, 1)
            hidden_low(2, 0)
            copy_T(3, 1)
            gelu(2, 0)
            with act.Fori(3, NT - 2, 2) as t:
                hidden_low(t, 1)
                copy_T(t + 1, 0)
                gelu(t, 1)
                hidden_low(t + 1, 0)
                copy_T(t + 2, 1)
                gelu(t + 1, 0)
            hidden_low(NT - 2, 1)
            copy_T(NT - 1, 0)
            gelu(NT - 2, 1)
            hidden_low(NT - 1, 0)
            gelu(NT - 1, 0)

        @block.vector
        def _(dve):
            V = nc.vector

            V.memset(pad[:, :], 0.0).then_inc(s_pad_zero, 1)
            dve.wait_ge(s_pad_zero, 1)
            dve.wait_ge(s_iotas, 4)
            V.tensor_scalar(pad[:, R_ID:R_ID + 1].bitcast(i32), tok[:, 0:1], TOK, None, ALU.add).then_inc(s_pad_made, 2)
            V.memset(Vh[:, :, :, :, D:D + 1], 1.0).then_inc(s_v_ones, 1)
            V.memset(rows[:, :, R_W + E:ROW], 0.0).then_inc(s_rows_zero, 1)
            V.memset(ones_row[:, :], 1.0).then_inc(s_ones_row, 1)
            V.memset(minus_half[:, :], -0.5).then_inc(s_minus_half, 1)
            V.memset(one8[:, :], 1.0).then_inc(s_table_const, 1)
            def split_router():
                dve.wait_ge(s_wr_in, 16)
                V.tensor_scalar(wr[:, 0, :, :], wr32[:, :, :], WS, None, ALU.mult).then_inc(s_router_split, 1)
                dve.wait_ge(s_router_split, 1)
                V.scalar_tensor_tensor(out=wr[:, 1, :, :], in0=wr32[:, :, :], scalar=WS, in1=wr[:, 0, :, :],
                                       op0=ALU.mult, op1=ALU.subtract).then_inc(s_router_split, 1)

            def w_low(e, c):
                n = NCH * e + c
                dve.wait_ge(s_w_high, n + 1)
                hi, lo = halves(e, c)
                V.scalar_tensor_tensor(out=lo, in0=staged(c, hi), scalar=WS, in1=hi,
                                       op0=ALU.mult, op1=ALU.subtract).then_inc(s_w_low, 1)

            def low_T(name, dst, first, high, b):
                dve.wait_ge(high, b + 1)
                ps = J_b[bank_of(name)][:, :].rearrange("p (c n) -> p c n", c=KC)
                for c in range(KC):
                    last = V.scalar_tensor_tensor(out=dst[:, 1, c, :], in0=ps[:, c, :], scalar=bqkv_s[:, first + c:first + c + 1],
                                                  in1=dst[:, 0, c, :], op0=ALU.add, op1=ALU.subtract)
                return last

            def norm_stats(src, st, m, root, by, steps, before):
                for j in range(JT):
                    last = V.bn_stats(st[:, j, :], src[:, j, :])
                last.then_inc(steps, 1)
                dve.wait_ge(steps, apart(dve, before + 1))
                for j in range(JT):
                    last = V.bn_aggr(m[:, j, :], st[:, j, :])
                last.then_inc(steps, 1)
                dve.wait_ge(steps, before + 2)
                V.tensor_scalar(by[:, :], m[:, :, 0], -1.0, None, ALU.mult)
                V.tensor_scalar(root[:, :], m[:, :, 1], EPS, None, ALU.add).then_inc(steps, 1)

            def head_maxima(b, i):
                dve.wait_ge(s_s_mm, H * b + i + 1)
                if i == 0:
                    if due(b):
                        dve.wait_ge(s_maxT_mm, b)
                V.tensor_reduce(mx[:, :].rearrange("p (s j h) -> p s j h", s=2, j=JT)[:, i % 2, :, i // 2],
                                S_b[i % 2], X, ALU.max).then_inc(s_max_done, 1)

            def step(t, static):
                b_a, b_s, b_c, b_d, b_e = stages(t, static)
                e = expert_of(t, static)
                for i in range(SLOTS):
                    if b_s is not None:
                        head_maxima(b_s, i)
                    b, h = head_at(i, LAG_ST, b_c, b_d)
                    if b is not None and h in ON_DVE:
                        dve.wait_ge(s_exp_done, H * b + h + 1)
                        p_low(V, h).then_inc(s_p_low_v, 1)
                    if b_e is not None:
                        if i == 1:
                            dve.wait_ge(s_logit_mm, b_e + 1)
                            V.tensor_scalar(lg[:, :, :], J_b[bank_of("logit")][:, 0:JT * E].rearrange(
                                "p (j e) -> p j e", j=JT), 1 / (XS * WS), None, ALU.mult).then_inc(s_logit_read, 1)
                            dve.wait_ge(s_logit_read, apart(dve, b_e + 1))
                            for j in range(JT):
                                last = V.max(top[:, j, :], lg[:, j, :])
                            last.then_inc(s_route_steps, 1)
                            dve.wait_ge(s_route_steps, apart(dve, ROUTE * b_e + 1))
                            for j in range(JT):
                                last = V.max_index(topi[:, j, :], top[:, j, :], lg[:, j, :])
                            last.then_inc(s_route_steps, 1)
                            if due(b_e):
                                dve.wait_ge(s_exp_gap, b_e)
                            V.tensor_tensor(gap[:, :], top[:, :, 1], top[:, :, 0], ALU.subtract).then_inc(s_gap, 1)
                            dve.wait_ge(s_route_steps, ROUTE * b_e + 2)
                            V.tensor_copy(topf[:, :, :], topi[:, :, 0:2]).then_inc(s_route_steps, 1)
                            dve.wait_ge(s_route_steps, ROUTE * b_e + 3)
                            V.tensor_tensor(
                                hot[:, :, :, :], expert_no[:, :].unsqueeze(1).unsqueeze(1).broadcast_to([P, JT, 2, E]),
                                topf[:, :, :].unsqueeze(3).broadcast_to([P, JT, 2, E]), ALU.is_equal).then_inc(s_route_steps, 1)
                            dve.wait_ge(s_route_steps, ROUTE * b_e + 4)
                            if due(b_e):
                                dve.wait_ge(s_rank_mm, b_e)
                            V.tensor_tensor(both[:, :, :], hot[:, :, 0, :], hot[:, :, 1, :], ALU.add).then_inc(
                                s_both_hot, 1)
                        if i == 4:
                            dve.wait_ge(s_exp_gap, b_e + 1)
                            V.tensor_scalar(den[:, :], eg[:, :], 1.0, None, ALU.add).then_inc(s_route_steps, 1)
                            dve.wait_ge(s_route_steps, ROUTE * b_e + 5)
                            V.reciprocal(wt[:, :, 0], den[:, :]).then_inc(s_route_steps, 1)
                            dve.wait_ge(s_route_steps, ROUTE * b_e + 6)
                            V.tensor_tensor(wt[:, :, 1], wt[:, :, 0], eg[:, :], ALU.mult).then_inc(s_pair_weight, 1)
                            dve.wait_ge(s_pair_weight, b_e + 1)
                            V.tensor_tensor(hw[:, :, :, :], hot[:, :, :, :],
                                            wt[:, :, :].unsqueeze(3).broadcast_to([P, JT, 2, E]), ALU.mult).then_inc(s_route_steps, 1)
                            dve.wait_ge(s_route_steps, ROUTE * b_e + 7)
                            V.tensor_tensor(rows[:, :, R_W:R_W + E], hw[:, :, 0, :], hw[:, :, 1, :], ALU.add).then_inc(s_route_steps, 1)
                            V.tensor_copy(rows[:, :, R_ID].bitcast(i32), tok[:, ds(b_e * JT, JT)]).then_inc(s_route_steps, 1)
                        if i == 6:
                            dve.wait_ge(s_rank_mm, b_e + 1)
                            if due(b_e):
                                dve.wait_ge(s_rank_read, b_e)
                            ps = J_b[bank_of("rank")]
                            V.tensor_tensor(pos8[:, :, :], ps[:, 0:JT * E].rearrange("p (j e) -> p j e", j=JT),
                                            base[:, :].unsqueeze(1).broadcast_to([P, JT, E]), ALU.add).then_inc(s_route_steps, 1)
                            dve.wait_ge(s_route_steps, ROUTE * b_e + 10)
                            V.tensor_tensor(base[:, :], ps[:, JT * E:(JT + 1) * E], base[:, :], ALU.add).then_inc(
                                s_rank_read, 1)
                            V.tensor_tensor(hp[:, :, :, :], hot[:, :, :, :],
                                            pos8[:, :, :].unsqueeze(2).broadcast_to([P, JT, 2, E]), ALU.mult).then_inc(s_route_steps, 1)
                            dve.wait_ge(s_route_steps, ROUTE * b_e + 11)
                            V.tensor_reduce(posf[:, :], hp[:, :, :, :].rearrange("p j k e -> p (j k) e"), X,
                                            ALU.add).then_inc(s_pos_f, 1)
                            dve.wait_ge(s_pos_f, b_e + 1)
                            if due(64 * b_e):
                                dve.wait_ge(s_scattered, 64 * b_e)
                            V.tensor_copy(pos[:, :], posf[:, :]).then_inc(s_pair_rows, 1)
                    if b_a is not None:
                        if i == 0:
                            dve.wait_ge(s_x_in, 16 * (b_a + 1))
                            if due(2 * b_a):
                                dve.wait_ge(s_xn_done, 2 * b_a)
                            norm_stats(x_in, stats, mv, rstd, shift, s_ln1_steps, 3 * b_a)
                        if i == 3:
                            low_T("k", k16, KC, s_k_high, b_a).then_inc(s_k_split, 1)
                        if i == 5:
                            dve.wait_ge(s_v_high, b_a + 1)
                            r = ds(b_a % VR, 1)
                            V.tensor_tensor(Vl[:, r, :, :, :].rearrange("p r j h d -> p (r j) h d"),
                                            J_b[bank_of("v")][:, :].rearrange("p (j h d) -> p j h d", j=JT, h=H),
                                            Vh[:, r, :, :, 0:D].rearrange("p r j h d -> p (r j) h d"),
                                            ALU.subtract).then_inc(s_v_split, 1)
                        if i == 9:
                            low_T("q", q16, 0, s_q_high, b_a).then_inc(s_q_split, 1)
                    if b_d is not None:
                        if i == 10:
                            dve.wait_ge(s_x1_mm, b_d + 1)
                            dve.wait_ge(s_x_res_in, 16 * (b_d + 1))
                            if due(16 * b_d):
                                dve.wait_ge(s_x1_out, 16 * b_d)
                            if due(LN2 * b_d):
                                dve.wait_ge(s_ln2_steps, LN2 * b_d)
                            V.tensor_tensor(x1[:, :, :], J_b[bank_of("x1")][:, :].rearrange("p (j c) -> p j c", j=JT),
                                            x_res[:, :, :], ALU.add).then_inc(s_x1_read, 1)
                            dve.wait_ge(s_x1_read, b_d + 1)
                            norm_stats(x1, stats2, mv2, rstd2, shift2, s_ln2_steps, LN2 * b_d)
                        if i == 13:
                            dve.wait_ge(s_xn2_done, 2 * (b_d + 1))
                            if due(64 * b_d):
                                dve.wait_ge(s_scattered, 64 * b_d)
                            dve.wait_ge(s_rows_zero, 1)
                            V.tensor_scalar(rows16[:, :, 0:C], xn2[:, :, :], XS, None, ALU.mult).then_inc(
                                s_row_high, 1)
                            dve.wait_ge(s_row_high, b_d + 1)
                            V.scalar_tensor_tensor(out=rows16[:, :, C:2 * C], in0=xn2[:, :, :], scalar=XS,
                                                   in1=rows16[:, :, 0:C], op0=ALU.mult, op1=ALU.subtract).then_inc(
                                s_row_parts, 1)
                    if e is not None and i - 1 in W_SLOTS:
                        w_low(e, W_SLOTS.index(i - 1))
                    b, h = head_at(i, LAG_PV, b_c, b_d)
                    if b is not None and h % 4 == 3:
                        g = h // 4
                        dve.wait_ge(s_pv_mm, H * b + 4 * g + 4)
                        if due(4 * b + g):
                            dve.wait_ge(s_o_read, 4 * b + g)
                        V.reciprocal(rsum[:, :, :], O_b[g % 2][:, :, :, D]).then_inc(s_sums_inverted, 1)
                        dve.wait_ge(s_sums_inverted, 4 * b + g + 1)
                        if g == 0:
                            if due(b):
                                dve.wait_ge(s_oT_mm, b)
                        V.tensor_tensor(o_n[:, :, g * 4 * D:(g + 1) * 4 * D].rearrange("p j (h d) -> p j h d", h=4),
                                        O_b[g % 2][:, :, :, 0:D],
                                        rsum[:, :, :].unsqueeze(3).broadcast_to([P, JT, 4, D]), ALU.mult).then_inc(
                            s_o_read, 1)
                    if static and t == 0 and i == 0:
                        V.memset(Ks, 1.0).then_inc(s_k_ones, 1)
                    if static and t == 0 and i == 6:
                        split_router()

            dve.wait_ge(s_iotas, 4)
            V.tensor_copy(base[:, :], region[:, :]).then_inc(s_base_set, 1)
            dve.wait_ge(s_base_set, 1)
            pipeline(dve, step)
            dve.wait_ge(s_rank_read, B)
            dve.wait_ge(s_table_const, 1)
            V.tensor_copy(pad_at[:, :], base[0:1, :]).then_inc(s_table, 1)
            V.scalar_tensor_tensor(out=tni[:, 0, :], in0=base[0:1, :], scalar=float(P - 1), in1=region[0:1, :],
                                        op0=ALU.add, op1=ALU.subtract).then_inc(s_table_steps, 1)
            dve.wait_ge(s_table_steps, 1)
            V.tensor_scalar(tni[:, 1, :], tni[:, 0, :], 7, None, ALU.arith_shift_right).then_inc(s_table_steps, 1)
            dve.wait_ge(s_table_steps, 2)
            V.tensor_copy(tn[:, :], tni[:, 1, :]).then_inc(s_table_steps, 1)
            dve.wait_ge(s_table_steps, 3)
            V.tensor_tensor_scan(tcum[:, :], one8[:, :], tn[:, :], 0.0, ALU.mult, ALU.add).then_inc(s_table_steps, 1)
            dve.wait_ge(s_table_steps, 4)
            V.tensor_tensor(tle[:, :, :], tcum[:, :].unsqueeze(1).broadcast_to([1, NT, E]),
                                 tix[:, :].unsqueeze(2).broadcast_to([1, NT, E]), ALU.is_le).then_inc(s_table_steps, 1)
            dve.wait_ge(s_table_steps, 5)
            V.tensor_reduce(tex[:, :], tle[:, :, :], X, ALU.add).then_inc(s_table_steps, 1)
            dve.wait_ge(s_table_steps, 6)
            V.tensor_tensor(tlx[:, :, :], tle[:, :, :], tn[:, :].unsqueeze(1).broadcast_to([1, NT, E]), ALU.mult).then_inc(s_table_steps, 1)
            dve.wait_ge(s_table_steps, 7)
            V.tensor_reduce(tskip[:, :], tlx[:, :, :], X, ALU.add).then_inc(s_table_steps, 1)
            dve.wait_ge(s_table_steps, 8)
            V.tensor_tensor(trow[:, :], tix[:, :], tskip[:, :], ALU.subtract).then_inc(s_table_steps, 1)
            dve.wait_ge(s_table_steps, 9)
            V.tensor_scalar(trow[:, :], trow[:, :], float(P), None, ALU.mult).then_inc(s_table_steps, 1)
            dve.wait_ge(s_table_steps, 10)
            V.scalar_tensor_tensor(out=trow[:, :], in0=tex[:, :], scalar=float(REG), in1=trow[:, :],
                                        op0=ALU.mult, op1=ALU.add).then_inc(s_table_steps, 1)
            dve.wait_ge(s_table_steps, 11)
            V.tensor_scalar(tr_i[:, :], trow[:, :], float(E * REG), None, ALU.min).then_inc(s_table, 1)
            V.tensor_scalar(te_i[:, :], tex[:, :], float(E - 1), None, ALU.min).then_inc(s_table, 1)
            dve.wait_ge(s_table, 3)

            for c in range(NCH):
                w_low(E - 1, c)

            def sum_hidden(t, p):
                for g in range(2):
                    dve.wait_ge(s_h_low, 2 * t + g + 1)
                    h = h32[:, p, 4 * g:4 * g + 4, :]
                    V.tensor_tensor(h, up_b[g][:, :, 0, :], h, ALU.add).then_inc(s_up_read, 1)

            def split_hidden(t, p):
                for g in range(2):
                    m = slice(4 * g, 4 * g + 4)
                    dve.wait_ge(s_gelu_done, MC * t + 4 * g + 4)
                    if g == 0:
                        if due(t - 1):
                            dve.wait_ge(s_down_mm, t - 1)
                    V.tensor_scalar(hh[:, p, m, :], h32[:, p, m, :], HS, None, ALU.mult).then_inc(s_h_high, 1)
                    dve.wait_ge(s_h_high, 2 * t + g + 1)
                    V.scalar_tensor_tensor(out=hl[:, p, m, :], in0=h32[:, p, m, :], scalar=HS, in1=hh[:, p, m, :],
                                           op0=ALU.mult, op1=ALU.subtract).then_inc(s_h_split, 1)

            def weigh(t, p):
                e = dve.value_load(te_i[0:1, ds(t, 1)], min_val=0, max_val=E - 1)
                dve.wait_ge(s_down_mm, t + 1)
                if due(t):
                    dve.wait_ge(s_y_weighted, t)
                V.scalar_tensor_tensor(out=y[:, 2, :], in0=bank[4 + p][:, 0:C], scalar=1 / (HS * WS),
                                       in1=b2_bc[:, ds(e, 1), :].rearrange("p e c -> p (e c)"),
                                       op0=ALU.mult, op1=ALU.add).then_inc(s_y_high, 1)
                dve.wait_ge(s_y_high, t + 1)
                V.scalar_tensor_tensor(out=y[:, 2, :], in0=bank[4 + p][:, C:2 * C], scalar=1 / (HS * WS), in1=y[:, 2, :],
                                       op0=ALU.mult, op1=ALU.add).then_inc(s_y_read, 1)
                dve.wait_ge(s_y_read, t + 1)
                dve.wait_ge(s_meta_in, 16 * (t + 1))
                if due(16 * (t - 1)):
                    dve.wait_ge(s_summed, 16 * (t - 1))
                V.tensor_scalar(y[:, p, :], y[:, 2, :], meta[:, p, ds(e + 1, 1)], None, ALU.mult).then_inc(
                    s_y_weighted, 1)

            dve.wait_ge(s_b2_in, 16)
            sum_hidden(0, 0)
            split_hidden(0, 0)
            sum_hidden(1, 1)
            weigh(0, 0)
            split_hidden(1, 1)
            sum_hidden(2, 0)
            weigh(1, 1)
            split_hidden(2, 0)
            with dve.Fori(3, NT - 2, 2) as t:
                sum_hidden(t, 1)
                weigh(t - 1, 0)
                split_hidden(t, 1)
                sum_hidden(t + 1, 0)
                weigh(t, 1)
                split_hidden(t + 1, 0)
            sum_hidden(NT - 2, 1)
            weigh(NT - 3, 0)
            split_hidden(NT - 2, 1)
            sum_hidden(NT - 1, 0)
            weigh(NT - 2, 1)
            split_hidden(NT - 1, 0)
            weigh(NT - 1, 0)

        @block.gpsimd
        def _(pool):
            G = nc.gpsimd
            G.iota(tok[:, :], pattern=[[P, TOK // P]], base=0, channel_multiplier=1).then_inc(s_iotas, 1)
            G.iota(expert_no[:, :], pattern=[[1, E]], base=0, channel_multiplier=0,
                   allow_small_or_imprecise_dtypes=True).then_inc(s_iotas, 1)
            G.iota(region[:, :], pattern=[[REG, E]], base=0, channel_multiplier=0,
                   allow_small_or_imprecise_dtypes=True).then_inc(s_iotas, 1)
            G.iota(tix[:, :], pattern=[[1, NT]], base=0, channel_multiplier=0,
                   allow_small_or_imprecise_dtypes=True).then_inc(s_iotas, 1)
            G.memset(id32[:, :], 0.0).then_inc(s_const_set, 1)
            G.memset(id16[:, :], 0.0).then_inc(s_const_set, 1)
            G.memset(tri[:, :], 1.0).then_inc(s_const_set, 1)
            G.memset(ones[:, :], 1.0).then_inc(s_consts, 1)
            pool.wait_ge(s_const_set, 3)
            for m in (id32, id16):
                G.affine_select(out=m[:, :], in_=m[:, :], compare_op=ALU.not_equal, fill=1.0, base=0,
                                pattern=[[-1, P]], channel_multiplier=1).then_inc(s_consts, 1)
            G.affine_select(out=tri[:, :], in_=tri[:, :], compare_op=ALU.is_gt, fill=0.0, base=0,
                            pattern=[[1, P]], channel_multiplier=-1).then_inc(s_consts, 1)


            def inverse_root(root, by, b, rooted, made):
                G.tensor_tensor(root[:, :], root[:, :], minus_half[:, :], ALU.pow).then_inc(rooted, 1)
                pool.wait_ge(rooted, apart(pool, b + 1))
                G.tensor_tensor(by[:, :], by[:, :], root[:, :], ALU.mult).then_inc(made, 1)

            def step(t, static):
                b_a, b_s, b_c, b_d, b_e = stages(t, static)
                for i in range(SLOTS):
                    b, h = head_at(i, LAG_ST, b_c, b_d)
                    if b is not None and h not in ON_DVE:
                        pool.wait_ge(s_exp_done, apart(pool, H * b + h + 1))
                        p_low(G, h).then_inc(s_p_low, 1)
                    if b_a is not None and i == 1:
                        pool.wait_ge(s_ln1_steps, apart(pool, 3 * b_a + 3))
                        pool.wait_ge(s_minus_half, 1)
                        inverse_root(rstd, shift, b_a, s_rooted, s_rstd)
                    if static and t == 0 and i == 1:
                        G.memset(Qs.bitcast(u32), 0).then_inc(s_q_zero, 1)
                    if b_d is not None and i == 11:
                        pool.wait_ge(s_ln2_steps, apart(pool, LN2 * b_d + 3))
                        inverse_root(rstd2, shift2, b_d, s_rooted2, s_rstd2)
                    if b_e is not None and 7 <= i < 7 + 2 * JT:
                        k = i - 7
                        if k == 0:
                            pool.wait_ge(s_pair_rows, apart(pool, b_e + 1))
                            pool.wait_ge(s_route_steps, apart(pool, ROUTE * (b_e + 1)))
                        G.indirect_dma_start(out=routed[:, :],
                                             out_offset=bass.IndirectOffsetOnAxis(ap=pos[:, k:k + 1], axis=0),
                                             in_=rows[:, k // 2, :], in_offset=None).then_inc(s_scattered, 16)

            pipeline(pool, step)

            def add_rows(t, p):
                pool.wait_ge(s_y_weighted, apart(pool, t + 1))
                if due(16 * t):
                    pool.wait_ge(s_summed, apart(pool, 16 * t))
                G.indirect_dma_start(out=acc[:, :],
                                     out_offset=bass.IndirectOffsetOnAxis(ap=meta[:, p, 0:1].bitcast(u32), axis=0),
                                     in_=y[:, p, :], in_offset=None, compute_op=ALU.add).then_inc(s_summed, 16)

            pool.wait_ge(s_x1_out, 16 * B)
            pool.wait_ge(s_acc_pad_out, 16)
            add_rows(0, 0)
            with pool.Fori(1, NT, 2) as t:
                add_rows(t, 1)
                add_rows(t + 1, 0)


_ARGS = ["x", "ctxT", "wqT", "wkT", "wvT", "woT", "bqkv", "bo", "wrT", "w12", "b1", "b2"]


def kernel(x, ctx_1024, L0_xattn_Wq, L0_xattn_bq, L0_xattn_Wk, L0_xattn_bk, L0_xattn_Wv, L0_xattn_bv, L0_xattn_Wo,
           L0_xattn_bo, L0_ffn_Wr, L0_ffn_W1, L0_ffn_b1, L0_ffn_W2, L0_ffn_b2):
    import numpy as np
    import concourse.bacc as bacc
    from concourse.bass_utils import run_bass_kernel_spmd

    def flat(a):
        return np.ascontiguousarray(a)

    def by_partition(a, *lead):
        return flat(np.moveaxis(np.asarray(a).reshape(*lead, -1, P), -1, 0).reshape(P, -1))

    w1 = np.asarray(L0_ffn_W1).transpose(0, 2, 1).reshape(E, KC, P, M).transpose(0, 2, 1, 3).reshape(E, P, KC * M)
    w2 = np.asarray(L0_ffn_W2).transpose(0, 2, 1).reshape(E, MC, P, C).transpose(0, 2, 1, 3).reshape(E, P, MC * C)
    arrays = {
        "x": flat(np.asarray(x).reshape(TOK, C)),
        "ctxT": flat(np.asarray(ctx_1024).transpose(0, 2, 1)),
        "wqT": flat(np.asarray(L0_xattn_Wq).T),
        "wkT": flat(np.asarray(L0_xattn_Wk).T),
        "wvT": flat(np.asarray(L0_xattn_Wv).T),
        "woT": flat(np.asarray(L0_xattn_Wo).T),
        "bqkv": flat(np.concatenate([by_partition(b) for b in (L0_xattn_bq, L0_xattn_bk, L0_xattn_bv)], 1)),
        "bo": flat(L0_xattn_bo),
        "wrT": flat(np.asarray(L0_ffn_Wr).T),
        "w12": flat(np.concatenate([w1, w2], 2)),
        "b1": by_partition(L0_ffn_b1, E),
        "b2": flat(L0_ffn_b2),
    }
    nc = bacc.Bacc("TRN2", target_bir_lowering=False, num_devices=1)
    args = [nc.dram_tensor(f"in_{n}", arrays[n].shape, mybir.dt.from_np(arrays[n].dtype), kind="ExternalInput").ap()
            for n in _ARGS]
    res = nc.dram_tensor("out_x", (B, N, C), mybir.dt.float32, kind="ExternalOutput").ap()
    cross_attention_moe(nc, *args, res)
    r = run_bass_kernel_spmd(nc, [{f"in_{n}": arrays[n] for n in _ARGS}], core_ids=[0])
    return r.results[0]["out_x"]
```
